# Optimizing a Trainium2 kernel written in Bass

```python
import numpy as np
import jax
import jax.numpy as jnp

def _softmax(x, axis=-1):
    return jax.nn.softmax(x, axis=axis)

def _gelu(x):
    return jax.nn.gelu(x, approximate=True)

def _silu(x):
    return jax.nn.silu(x)

def _sigmoid(x):
    return jax.nn.sigmoid(x)

def _layernorm(x, axis=-1, eps=1e-05):
    m = jnp.mean(x, axis=axis, keepdims=True)
    v = jnp.var(x, axis=axis, keepdims=True)
    return (x - m) / jnp.sqrt(v + eps)

def _scatter_add(tgt, idx, src, axis=0):
    return tgt.at[idx].add(src)

def _segment_sum(src, seg, n):
    return jax.ops.segment_sum(src, seg, n)
kernel_name = 'mk_sandwich_d1_jaxref_r8_dd7f74'

def setup_inputs(seed: int=0):
    np.random.seed(seed)
    _w = jnp.asarray

    def _L0_attn_setup():
        import math
        import jax, jax.numpy as jnp
        import numpy as np
        B, T, C = (2, 256, 128)
        HEADS = 16
        HD = C // HEADS

        def _rope_tables(seq_len, dim):
            pos = jnp.arange(seq_len, dtype=jnp.float32)
            freqs = 1.0 / 10000.0 ** (jnp.arange(0, dim, 2, dtype=jnp.float32) / dim)
            ang = pos[:, None] * freqs[None, :]
            return (jnp.sin(ang)[None, :, None, :], jnp.cos(ang)[None, :, None, :])

        def _apply_rope(t, sin, cos, dim):
            t1, t2 = (t[..., :dim // 2], t[..., dim // 2:])
            return jnp.concatenate([t1 * cos + t2 * sin, t1 * sin - t2 * cos], axis=-1)
        key = jax.random.key(seed)
        ks = jax.random.split(key, 5)
        s = 0.02
        return {'x': jax.random.normal(ks[0], (B, T, C), jnp.float32), 'Wq': jax.random.normal(ks[1], (C, C), jnp.float32) * s, 'bq': jnp.zeros((C,), jnp.float32), 'Wk': jax.random.normal(ks[2], (C, HD), jnp.float32) * s, 'bk': jnp.zeros((HD,), jnp.float32), 'Wv': jax.random.normal(ks[3], (C, HD), jnp.float32) * s, 'bv': jnp.zeros((HD,), jnp.float32), 'Wo': jax.random.normal(ks[4], (C, C), jnp.float32) * s, 'bo': jnp.zeros((C,), jnp.float32)}
    _L0_attn_in = _L0_attn_setup()

    def _L0_ffn_setup():
        import jax, jax.numpy as jnp
        import numpy as np
        D = 128
        F = 128
        E = 8
        K = 2
        B, T = (2, 256)

        def _moe_forward(x, router_w, w1, w2, shared_gate_up, shared_down, shared_gate_w):
            b, t, d = x.shape
            xf = x.reshape(-1, d)
            n = xf.shape[0]
            logits = xf @ router_w
            probs = jax.nn.softmax(logits, axis=-1)
            topw, topi = jax.lax.top_k(probs, K)
            combine = jnp.zeros((n, E), dtype=probs.dtype).at[jnp.arange(n)[:, None], topi].add(topw)
            h = jax.nn.silu(jnp.einsum('nd,edf->nef', xf, w1))
            ye = jnp.einsum('nef,efd->ned', h, w2)
            routed = jnp.einsum('ne,ned->nd', combine, ye)
            gu = xf @ shared_gate_up
            gate, up = (gu[:, :F], gu[:, F:])
            shared = jax.nn.silu(gate) * up @ shared_down
            shared = jax.nn.sigmoid(xf @ shared_gate_w) * shared
            return (routed + shared).reshape(b, t, d)
        key = jax.random.key(seed)
        ks = jax.random.split(key, 7)
        std = 0.02
        x = jax.random.normal(ks[0], (B, T, D), dtype=jnp.float32)
        router_w = jax.random.normal(ks[1], (D, E), dtype=jnp.float32) * std
        w1 = jax.random.normal(ks[2], (E, D, F), dtype=jnp.float32) * std
        w2 = jax.random.normal(ks[3], (E, F, D), dtype=jnp.float32) * std
        shared_gate_up = jax.random.normal(ks[4], (D, 2 * F), dtype=jnp.float32) * std
        shared_down = jax.random.normal(ks[5], (F, D), dtype=jnp.float32) * std
        shared_gate_w = jax.random.normal(ks[6], (D, 1), dtype=jnp.float32) * std
        return {'x': x, 'router_w': router_w, 'w1': w1, 'w2': w2, 'shared_gate_up': shared_gate_up, 'shared_down': shared_down, 'shared_gate_w': shared_gate_w}
    _L0_ffn_in = _L0_ffn_setup()
    _d = {'L0_attn_x': _L0_attn_in['x'], 'L0_attn_Wq': _L0_attn_in['Wq'], 'L0_attn_bq': _L0_attn_in['bq'], 'L0_attn_Wk': _L0_attn_in['Wk'], 'L0_attn_bk': _L0_attn_in['bk'], 'L0_attn_Wv': _L0_attn_in['Wv'], 'L0_attn_bv': _L0_attn_in['bv'], 'L0_attn_Wo': _L0_attn_in['Wo'], 'L0_attn_bo': _L0_attn_in['bo'], 'L0_ffn_router_w': _L0_ffn_in['router_w'], 'L0_ffn_w1': _L0_ffn_in['w1'], 'L0_ffn_w2': _L0_ffn_in['w2'], 'L0_ffn_shared_gate_up': _L0_ffn_in['shared_gate_up'], 'L0_ffn_shared_down': _L0_ffn_in['shared_down'], 'L0_ffn_shared_gate_w': _L0_ffn_in['shared_gate_w']}
    _x0 = _d['L0_attn_x']
    _d['L0_attn_x'] = jax.random.normal(jax.random.fold_in(jax.random.key(seed), 1), (4, 1024, 128), dtype=_x0.dtype)
    del _x0
    return _d

def reference(L0_attn_x, L0_attn_Wq, L0_attn_bq, L0_attn_Wk, L0_attn_bk, L0_attn_Wv, L0_attn_bv, L0_attn_Wo, L0_attn_bo, L0_ffn_router_w, L0_ffn_w1, L0_ffn_w2, L0_ffn_shared_gate_up, L0_ffn_shared_down, L0_ffn_shared_gate_w):

    def _L0_attn_ref(x, Wq, bq, Wk, bk, Wv, bv, Wo, bo):
        import math
        import jax, jax.numpy as jnp
        import numpy as np
        B, T, C = (2, 256, 128)
        HEADS = 16
        HD = C // HEADS

        def _rope_tables(seq_len, dim):
            pos = jnp.arange(seq_len, dtype=jnp.float32)
            freqs = 1.0 / 10000.0 ** (jnp.arange(0, dim, 2, dtype=jnp.float32) / dim)
            ang = pos[:, None] * freqs[None, :]
            return (jnp.sin(ang)[None, :, None, :], jnp.cos(ang)[None, :, None, :])

        def _apply_rope(t, sin, cos, dim):
            t1, t2 = (t[..., :dim // 2], t[..., dim // 2:])
            return jnp.concatenate([t1 * cos + t2 * sin, t1 * sin - t2 * cos], axis=-1)
        Bx, Tx, Cx = x.shape
        q = (x @ Wq + bq).reshape(Bx, Tx, HEADS, HD)
        k = (x @ Wk + bk)[:, :, None, :]
        v = (x @ Wv + bv)[:, :, None, :]
        sin, cos = _rope_tables(Tx, HD)
        q = _apply_rope(q, sin, cos, HD)
        k = _apply_rope(k, sin, cos, HD)
        att = jnp.einsum('bthd,bThd->bhtT', q, k) / math.sqrt(HD)
        causal = jnp.triu(jnp.ones((Tx, Tx), bool), 1)
        att = jnp.where(causal, -jnp.inf, att)
        att = jax.nn.softmax(att, axis=-1)
        out = jnp.einsum('bhtT,bThd->bthd', att, v).reshape(Bx, Tx, Cx)
        return out @ Wo + bo

    def _L0_ffn_ref(x, router_w, w1, w2, shared_gate_up, shared_down, shared_gate_w):
        import jax, jax.numpy as jnp
        import numpy as np
        D = 128
        F = 128
        E = 8
        K = 2
        B, T = (2, 256)

        def _moe_forward(x, router_w, w1, w2, shared_gate_up, shared_down, shared_gate_w):
            b, t, d = x.shape
            xf = x.reshape(-1, d)
            n = xf.shape[0]
            logits = xf @ router_w
            probs = jax.nn.softmax(logits, axis=-1)
            topw, topi = jax.lax.top_k(probs, K)
            combine = jnp.zeros((n, E), dtype=probs.dtype).at[jnp.arange(n)[:, None], topi].add(topw)
            h = jax.nn.silu(jnp.einsum('nd,edf->nef', xf, w1))
            ye = jnp.einsum('nef,efd->ned', h, w2)
            routed = jnp.einsum('ne,ned->nd', combine, ye)
            gu = xf @ shared_gate_up
            gate, up = (gu[:, :F], gu[:, F:])
            shared = jax.nn.silu(gate) * up @ shared_down
            shared = jax.nn.sigmoid(xf @ shared_gate_w) * shared
            return (routed + shared).reshape(b, t, d)
        return _moe_forward(x, router_w, w1, w2, shared_gate_up, shared_down, shared_gate_w)
    x = L0_attn_x
    x = x + _layernorm(_L0_attn_ref(_layernorm(x, axis=-1), L0_attn_Wq, L0_attn_bq, L0_attn_Wk, L0_attn_bk, L0_attn_Wv, L0_attn_bv, L0_attn_Wo, L0_attn_bo), axis=-1)
    x = x + _layernorm(_L0_ffn_ref(_layernorm(x, axis=-1), L0_ffn_router_w, L0_ffn_w1, L0_ffn_w2, L0_ffn_shared_gate_up, L0_ffn_shared_down, L0_ffn_shared_gate_w), axis=-1)
    return x

_drawn_inputs = setup_inputs


def setup_inputs(seed=0):
    import zlib

    import numpy as np

    out = dict(_drawn_inputs(seed))
    spreads = {'L0_attn_bq': (0.0, 0.607),
     'L0_attn_bk': (0.0, 0.8),
     'L0_attn_bv': (0.0, 0.1),
     'L0_attn_bo': (0.0, 0.1)}
    factors = {'L0_attn_Wq': 5.512, 'L0_attn_Wk': 3.172}
    for name, (base, spread) in spreads.items():
        noise = np.random.default_rng([zlib.crc32(name.encode()), seed]).standard_normal(out[name].shape)
        drawn = base * np.exp(spread * noise) if base else spread * noise
        out[name] = jnp.asarray(drawn.astype(out[name].dtype))
    for name, factor in factors.items():
        out[name] = (out[name] * factor).astype(out[name].dtype)
    return out
```

```python
from contextlib import ExitStack

import numpy as np

import concourse.bass as bass
from concourse import mybir

F32 = mybir.dt.float32
BF16 = mybir.dt.bfloat16
ALU = mybir.AluOpType
ACT = mybir.ActivationFunctionType
AX = mybir.AxisListType

P = 128
B, T, C = 4, 1024, 128
H, D = 16, 8
E = 8
G = E + 1
NT = T // P
QC = 32
NV = 1 + P // QC
BANK = 512
HALF = T // 2
PARTS = 3
ROW_MAX = PARTS * PARTS * D
ROW_MASK = 96
MASKED = -1e30
EPS = 1e-5
VW = 32
PSLOTS = 3

BT = 512 // P


def maximum_pieces():
    pieces = []
    for i in range(NT):
        lo, hi = BANK * (i // BT), P * (i + 1)
        if lo:
            pieces += [(i, [h], 0, lo) for h in range(H)]
        n = BANK // (hi - lo)
        pieces += [(i, list(range(h, h + n)), lo, hi) for h in range(0, H, n)]
    return pieces


PIECES = maximum_pieces()
NPIECE = len(PIECES)
STEPS = [(i, kt) for i in range(NT) for kt in range(i + 1)]
NSTEP = len(STEPS)


def attention_order():
    pieces = [[n for n, p in enumerate(PIECES) if p[0] == i] for i in range(NT)]
    order = [("M", m) for m in pieces[0] + pieces[1]] + [("T", 0), ("T", 1)]
    n = 0
    for i in range(NT):
        ahead = pieces[i + 2] if i + 2 < NT else []
        for kt in range(i + 1):
            order.append(("S", n))
            lo, hi = len(ahead) * kt // (i + 1), len(ahead) * (kt + 1) // (i + 1)
            order += [("M", m) for m in ahead[lo:hi]]
            if kt == 0 and 1 <= i < NT - 1:
                order.append(("T", i + 1))
            if n:
                order.append(("V", n - 1))
            n += 1
    return order + [("V", NSTEP - 1)]


ORDER = attention_order()


def build(nc, x, w_in, w_out, b_q, b_kv, b_o, rope_q, rope_k, w_router, w_up, w_down, w_gu, w_sd, out):
    with ExitStack() as ctx:
        def sb(name, shape, dt=F32):
            return ctx.enter_context(nc.sbuf_tensor(name, shape, dt))

        def pb(name, shape, dt=F32):
            return ctx.enter_context(nc.psum_tensor(name, shape, dt))

        def sem(name):
            return ctx.enter_context(nc.semaphore(name))

        q_scr = nc.dram_tensor("q_scr", (PARTS, P, T), BF16, kind="Internal").ap()
        num_scr = nc.dram_tensor("num_scr", (P, T), F32, kind="Internal").ap()
        den_scr = nc.dram_tensor("den_scr", (P, T), F32, kind="Internal").ap()

        wi = sb("wi", [P, 2 * C + 3 * D])
        wo = sb("wo", [P, C])
        bq = sb("bq", [P, 2])
        bkv = sb("bkv", [P, 3, D])
        bo = sb("bo", [P, C])
        ropq = sb("ropq", [P, 2, T])
        ropk = sb("ropk", [P, 2, NT, D])
        wr = sb("wr", [P, G])
        w1 = sb("w1", [P, E, C])
        w2 = sb("w2", [P, E, C])
        wgu = sb("wgu", [P, 2 * C])
        wsd = sb("wsd", [P, C])
        tri = sb("tri", [P, P], BF16)
        ident = sb("ident", [P, P])
        identb = sb("identb", [P, P], BF16)
        half_pow = sb("half_pow", [P, NT])
        rank = sb("rank", [P, NT, E])
        zrow = sb("zrow", [P, T], BF16)

        xt = sb("xt", [P, NT, C])
        xh = sb("xh", [P, NT, C])
        xT = sb("xT", [P, T])
        stat = sb("stat", [P, NT, 6])
        mv = sb("mv", [P, NT, 2])
        veps = sb("veps", [P, NT])
        rstd = sb("rstd", [P, NT])
        qa = sb("qa", [P, T])
        qb = sb("qb", [P, T])
        qr = sb("qr", [P, T])
        qp = sb("qp", [P, PARTS, T], BF16)
        ka = sb("ka", [P, NT, D])
        kb = sb("kb", [P, NT, D])
        kr = sb("kr", [P, NT, D])
        kp = sb("kp", [P, NT, PARTS, PARTS, D], BF16)
        vx = sb("vx", [P, NT, VW])
        QT = sb("QT", [P, H, T], BF16)
        KT = sb("KT", [P, NV, T], BF16)
        nmx = sb("nmx", [P, NT, H])
        nmx2 = sb("nmx2", [P, NT // 2, 2, H])
        nm = sb("nm", [H, 2, P])
        nmr = sb("nmr", [H, 2, P])
        nmp = sb("nmp", [H, 2, PARTS, P], BF16)
        pT = sb("pT", [P, PSLOTS, 4, BANK])
        osb = sb("osb", [P, 2, BANK])
        oT = sb("oT", [P, T])
        dT = sb("dT", [P, T])
        rD = sb("rD", [P, T])
        aT = sb("aT", [P, T])

        xr = sb("xr", [P, NT, C])
        y = sb("y", [P, NT, C])
        x1 = sb("x1", [P, NT, C])
        xh2 = sb("xh2", [P, NT, C])
        x2T = sb("x2T", [P, T])
        ostat = sb("ostat", [P, NT, 6])
        omv = sb("omv", [P, NT, 2])
        oveps = sb("oveps", [P, NT])
        orstd = sb("orstd", [P, NT])
        lg = sb("lg", [P, NT, G])
        ls = sb("ls", [P, NT, E])
        ex = sb("ex", [P, NT, E])
        eg = sb("eg", [P, NT])
        pr = sb("pr", [P, NT, E])
        p2 = sb("p2", [P, NT, E])
        eq = sb("eq", [P, NT, E])
        cand = sb("cand", [P, NT, E])
        oh1 = sb("oh1", [P, NT, E])
        oh2 = sb("oh2", [P, NT, E])
        red = sb("red", [P, NT, 1])
        cmb = sb("cmb", [P, G, NT])
        cT = sb("cT", [G * NT, P])
        crow = sb("crow", [P, 3, T])
        cb = sb("cb", [P, 3, BANK])
        hsil = sb("hsil", [P, 3, BANK])
        hs = sb("hs", [P, 3, BANK])
        shd = sb("shd", [P, BANK])

        psS = pb("psS", [P, 4, BANK])
        psM = pb("psM", [P, 2, BANK])
        psO = pb("psO", [P, BANK])
        psX = pb("psX", [P, BANK])
        psOb = psO[:, :].bitcast(BF16)

        s = {n: sem(n) for n in (
            "w_loaded", "const_v", "const_p", "x_loaded", "xr_loaded",
            "ln1_stat", "ln1_mv", "ln1_veps", "ln1_rstd", "ln1_out", "xT_ps", "xT_act", "xT_dve",
            "q_ps", "kv_ps", "kT_ps", "qa_done", "qb_done", "q_steps", "k_steps", "v_done", "kT_done",
            "q_scr_done", "q_rows",
            "m_ps", "m_max", "m_block", "nmT_ps", "nm_copied", "nm_steps", "nm_rows0", "nm_rows1",
            "s_ps", "exp_done", "pv_done", "o_evac", "o_written0", "o_written1", "o_read0", "o_read1", "den_inv", "a_done",
            "pj_ps", "y_done", "lnO_stat", "lnO_mv", "lnO_veps", "lnO_rstd", "yn_done", "x1_done", "xh2_done",
            "x2T_ps", "x2T_act", "x2T_dve", "rt_ps", "rt_steps", "ls_done", "ex_done", "cmb_done", "cT_ps", "cT_done",
            "crow_done", "cb_done", "h_ps", "silu_done", "shd_done", "hs_done", "ye_ps", "yo_done", "out_done", "stored", "passed")}

        xb = x.rearrange("b (i p) c -> b p i c", p=P)
        ob = out.rearrange("b (i p) c -> b p i c", p=P)
        num_h = num_scr.rearrange("(h d) t -> d h t", d=D)
        den_h = den_scr.rearrange("(h d) t -> d h t", d=D)
        N_O = NT // 2 * 8 * 16
        N_Q = 10 * 16
        def apart(eng, sem_name, value):
            eng.wait_ge(s[sem_name], 1 + value)
            eng.sem_inc(s["passed"], 1)

        names = list(s)
        with nc.Block() as start:
            for n, on in enumerate((start.sync, start.scalar, start.tensor, start.vector, start.gpsimd)):
                @on
                def _(eng, n=n):
                    for name in names[n::5]:
                        eng.sem_inc(s[name], 1)

        block = ctx.enter_context(nc.Block())

        @block.sync
        def _(sp):
            weights = [(wi[:, :], w_in), (ropq[:, :, :], rope_q), (ropk[:, :, :, :], rope_k),
                       (bq[:, :], b_q), (bkv[:, :, :], b_kv), (bo[:, :], b_o), (wo[:, :], w_out), (wr[:, :], w_router),
                       (w1[:, :, :], w_up.rearrange("e d f -> d e f")), (w2[:, :, :], w_down.rearrange("e f d -> f e d")),
                       (wgu[:, :], w_gu), (wsd[:, :], w_sd)]

            def load_x(b):
                apart(sp, "ln1_out", NT * b)
                sp.dma_start(xt[:, :, :], xb[b]).then_inc(s["x_loaded"], 16)

            def a_stage(b):
                sp.wait_ge(s["q_steps"], 1 + 5 * b + 5)
                sp.dma_start(q_scr.rearrange("a p t -> p a t"), qp[:, :, :]).then_inc(s["q_scr_done"], 16)
                sp.wait_ge(s["pv_done"], 1 + NSTEP * b)
                sp.dma_start(QT[ROW_MAX:ROW_MAX + PARTS, :, :],
                             zrow[0:PARTS, :].unsqueeze(1).to_broadcast([PARTS, H, T])).then_inc(s["q_rows"], 16)
                sp.wait_ge(s["q_scr_done"], 1 + 16 * b + 16)
                for a in range(PARTS):
                    for k in range(PARTS):
                        r = (PARTS * a + k) * D
                        sp.dma_start(QT[r:r + D, :, :],
                                     q_scr[a].rearrange("(h j) t -> j h t", j=D)).then_inc(s["q_rows"], 16)

            def nm_rows(b, i):
                sp.wait_ge(s["nm_steps"], 1 + 4 * (NT * b + i) + 4)
                for a in range(PARTS):
                    sp.dma_start(QT[ROW_MAX + a:ROW_MAX + a + 1, :, P * i:P * (i + 1)],
                                 nmp[:, i % 2, a, :]).then_inc(s[f"nm_rows{i % 2}"], 16)

            def o_write(b, i):
                sp.wait_ge(s["o_evac"], 1 + NT * b + i + 1)
                for r in range(4):
                    t0 = P * i + QC * r
                    for w, scr in ((0, num_h), (D, den_h)):
                        sp.dma_start(scr[:, :, t0:t0 + QC],
                                     osb[32 * r + w:32 * r + w + D, i % 2, :].rearrange("d (h t) -> d h t", h=H)
                                     ).then_inc(s[f"o_written{i % 2}"], 16)

            def o_read(b, c):
                for w in range(2):
                    sp.wait_ge(s[f"o_written{w}"], 1 + N_O * b + (N_O // 2) * (c + 1))
                sp.dma_start(oT[:, HALF * c:HALF * (c + 1)], num_scr[:, HALF * c:HALF * (c + 1)]).then_inc(s[f"o_read{c}"], 16)
                sp.dma_start(dT[:, HALF * c:HALF * (c + 1)], den_scr[:, HALF * c:HALF * (c + 1)]).then_inc(s[f"o_read{c}"], 16)

            def mp_stage(b):
                for c in range(2):
                    apart(sp, f"o_read{c}", 32 * b)
                sp.wait_ge(s["a_done"], 1 + 2 * b)
                for what, n in ORDER:
                    if what == "T":
                        nm_rows(b, n)
                    elif what == "V" and STEPS[n][0] == STEPS[n][1]:
                        i = STEPS[n][0]
                        o_write(b, i)
                        if i % 4 == 3:
                            o_read(b, i // 4)

            def o_stage(b):
                apart(sp, "x1_done", b)
                sp.dma_start(xr[:, :, :], xb[b]).then_inc(s["xr_loaded"], 16)
                sp.wait_ge(s["cT_done"], 1 + b + 1)
                for e in range(G):
                    sp.dma_start(crow[32 * (e % 4):32 * (e % 4) + 1, e // 4, :].rearrange("o (i t) -> o i t", t=P),
                                 cT[NT * e:NT * (e + 1), :]).then_inc(s["crow_done"], 16)
                apart(sp, "out_done", b + 1)
                sp.dma_start(ob[b], y[:, :, :]).then_inc(s["stored"], 16)

            load_x(0)
            for dst, src in weights:
                sp.dma_start(dst, src).then_inc(s["w_loaded"], 16)
            sp.wait_ge(s["const_v"], 1 + 3)
            a_stage(0)
            with sp.Fori(0, B - 1) as b:
                load_x(b + 1)
                mp_stage(b)
                a_stage(b + 1)
                o_stage(b)
            mp_stage(B - 1)
            o_stage(B - 1)
            sp.wait_ge(s["stored"], 1 + 16 * B)

        NW = 12 * 16

        NCP = 8 + NV - 1 + 1

        @block.gpsimd
        def _(pool):
            pool.memset(ident[:, :], 0.0).then_inc(s["const_p"], 1)
            pool.memset(identb[:, :], 0.0).then_inc(s["const_p"], 1)
            pool.memset(tri[:, :], 0.0).then_inc(s["const_p"], 1)
            pool.memset(half_pow[:, :], -0.5).then_inc(s["const_p"], 1)
            pool.wait_ge(s["const_p"], 1 + 4)
            pool.affine_select(out=ident[:, :], in_=ident[:, :], compare_op=ALU.not_equal, fill=1.0,
                               base=0, pattern=[[-1, P]], channel_multiplier=1).then_inc(s["const_p"], 1)
            pool.affine_select(out=identb[:, :], in_=identb[:, :], compare_op=ALU.not_equal, fill=1.0,
                               base=0, pattern=[[-1, P]], channel_multiplier=1).then_inc(s["const_p"], 1)
            pool.affine_select(out=tri[:, :], in_=tri[:, :], compare_op=ALU.is_ge, fill=MASKED,
                               base=0, pattern=[[-1, P]], channel_multiplier=1).then_inc(s["const_p"], 1)
            pool.iota(rank[:, :, :], pattern=[[0, NT], [-1, E]], base=E, channel_multiplier=0,
                      allow_small_or_imprecise_dtypes=True).then_inc(s["const_p"], 1)

            def rstd_of(b, n, k, var, ve, rs, mv_sem, ve_sem, rs_sem):
                apart(pool, mv_sem, NT * (n * b + k + 1))
                pool.tensor_scalar(ve, var, EPS, None, ALU.add).then_inc(s[ve_sem], 1)
                pool.wait_ge(s[ve_sem], 1 + n * b + k + 1)
                pool.tensor_tensor(rs, ve, half_pow[:, :], ALU.pow).then_inc(s[rs_sem], 1)

            def ln1(b):
                rstd_of(b, 1, 0, mv[:, :, 1], veps[:, :], rstd[:, :], "ln1_mv", "ln1_veps", "ln1_rstd")

            def split_max(b, i):
                n = 4 * (NT * b + i)
                src, rest, part = nm[:, i % 2, :], nmr[:, i % 2, :], nmp[:, i % 2, :, :]
                pool.wait_ge(s[f"nm_rows{i % 2}"], 1 + 48 * (NT // 2 * b + i // 2))
                pool.wait_ge(s["nm_steps"], 1 + n)
                apart(pool, "nm_copied", NT * b + i + 1)
                pool.tensor_copy(part[:, 0, :], src).then_inc(s["nm_steps"], 1)
                pool.wait_ge(s["nm_steps"], 1 + n + 1)
                pool.tensor_tensor(rest, src, part[:, 0, :], ALU.subtract).then_inc(s["nm_steps"], 1)
                apart(pool, "nm_steps", n + 2)
                pool.tensor_copy(part[:, 1, :], rest).then_inc(s["nm_steps"], 1)
                pool.wait_ge(s["nm_steps"], 1 + n + 3)
                pool.tensor_tensor(part[:, 2, :], rest, part[:, 1, :], ALU.subtract).then_inc(s["nm_steps"], 1)

            def mp_stage(b):
                pool.wait_ge(s["lnO_rstd"], 1 + 3 * b)
                for what, n in ORDER:
                    if what == "T":
                        split_max(b, n)
                pool.wait_ge(s["nm_steps"], 1 + 4 * NT * (b + 1))

            def o_stage(b):
                for k in range(2):
                    if k:
                        pool.wait_ge(s["lnO_rstd"], 1 + 3 * b + 1)
                    rstd_of(b, 3, k, omv[:, :, 1], oveps[:, :], orstd[:, :], "lnO_mv", "lnO_veps", "lnO_rstd")
                pool.wait_ge(s["lnO_rstd"], 1 + 3 * b + 2)
                pool.wait_ge(s["crow_done"], 1 + G * 16 * (b + 1))
                for c in range(2):
                    for e in range(G):
                        k = G * c + e
                        pool.wait_ge(s["cb_done"], 1 + 2 * G * b + k)
                        apart(pool, "hs_done", 2 * G * b + max(k - 2, 0))
                        pool.partition_broadcast(cb[:, k % 3, :],
                                                 crow[32 * (e % 4):32 * (e % 4) + 1, e // 4, HALF * c:HALF * (c + 1)],
                                                 P).then_inc(s["cb_done"], 1)
                pool.wait_ge(s["cb_done"], 1 + 2 * G * (b + 1))
                rstd_of(b, 3, 2, omv[:, :, 1], oveps[:, :], orstd[:, :], "lnO_mv", "lnO_veps", "lnO_rstd")

            ln1(0)
            pool.wait_ge(s["const_v"], 1 + 3)
            pool.wait_ge(s["ln1_rstd"], 1 + 1)
            for v in range(1, NV):
                m = KT[ROW_MASK:P, v, :].rearrange("p (i k) -> p i k", k=P)
                pool.affine_select(out=m, in_=m, compare_op=ALU.is_ge, fill=MASKED, base=QC * (v - 1),
                                   pattern=[[0, NT], [-1, P]], channel_multiplier=1).then_inc(s["const_p"], 1)
                pool.wait_ge(s["const_p"], 1 + 8 + v)
            m = QT[ROW_MASK:P, :, :].rearrange("p h (c t) -> p (h c) t", t=QC)
            pool.affine_select(out=m, in_=m, compare_op=ALU.not_equal, fill=1.0, base=0,
                               pattern=[[0, H * T // QC], [1, QC]], channel_multiplier=-1).then_inc(s["const_p"], 1)
            pool.wait_ge(s["const_p"], 1 + NCP)
            with pool.Fori(0, B - 1) as b:
                mp_stage(b)
                ln1(b + 1)
                pool.wait_ge(s["ln1_rstd"], 1 + b + 2)
                o_stage(b)
            mp_stage(B - 1)
            o_stage(B - 1)


        @block.scalar
        def _(act):
            def a_stage(b):
                act.wait_ge(s["xT_ps"], 1 + 2 * b + 1)
                nc.scalar.activation(xT[:, 0:HALF], psS[:, 0, :], ACT.Copy).then_inc(s["xT_act"], 1)

            def mp_stage(b):
                for what, n in ORDER:
                    if what != "S":
                        continue
                    if n >= PSLOTS:
                        act.wait_ge(s["pv_done"], 1 + NSTEP * b + n - PSLOTS + 1)
                    else:
                        act.wait_ge(s["pv_done"], 1 + NSTEP * b)
                    for u in range(2):
                        act.wait_ge(s["s_ps"], 1 + 2 * (NSTEP * b + n) + u + 1)
                        nc.scalar.activation(pT[:, n % PSLOTS, 2 * u:2 * u + 2, :], psS[:, 2 * u:2 * u + 2, :],
                                             ACT.Exp, scale=float(D) ** -0.5).then_inc(s["exp_done"], 1)

            def o_stage(b):
                act.wait_ge(s["x2T_ps"], 1 + 2 * b + 1)
                nc.scalar.activation(x2T[:, 0:HALF], psS[:, 2, :], ACT.Copy).then_inc(s["x2T_act"], 1)
                act.wait_ge(s["ls_done"], 1 + b + 1)
                nc.scalar.activation(ex[:, :, :], ls[:, :, :], ACT.Exp).then_inc(s["ex_done"], 1)
                nc.scalar.activation(eg[:, :], lg[:, :, E], ACT.Exp, scale=-1.0).then_inc(s["ex_done"], 1)
                for c in range(2):
                    for e in range(G):
                        k = G * c + e
                        bank = ((G + 1) * c + e) % 4
                        act.wait_ge(s["h_ps"], 1 + 2 * G * b + k + 1)
                        if k >= 3:
                            act.wait_ge(s["hs_done"], 1 + 2 * G * b + k - 2)
                        else:
                            act.wait_ge(s["hs_done"], 1 + 2 * G * b)
                        nc.scalar.activation(hsil[:, k % 3, :], psS[:, bank, :], ACT.Silu).then_inc(s["silu_done"], 1)

            a_stage(0)
            with act.Fori(0, B - 1) as b:
                mp_stage(b)
                a_stage(b + 1)
                o_stage(b)
            mp_stage(B - 1)
            o_stage(B - 1)

        @block.tensor
        def _(pe):
            mm = nc.tensor.matmul

            def a_stage(b):
                pe.wait_ge(s["o_evac"], 1 + NT * b)
                for i in range(NT):
                    pe.wait_ge(s["ln1_out"], 1 + NT * b + i + 1)
                    t = pe.transpose(psS[:, i // 4, P * (i % 4):P * (i % 4 + 1)], xh[:, i, :], ident[:, :])
                    if i % 4 == 3:
                        t.then_inc(s["xT_ps"], 1)
                pe.wait_ge(s["xT_act"], 1 + b + 1)
                pe.wait_ge(s["xT_dve"], 1 + b + 1)
                for w in range(2):
                    for c in range(2):
                        q = mm(psS[:, 2 * (1 - w) + c, :], wi[:, C * w:C * (w + 1)], xT[:, HALF * c:HALF * (c + 1)],
                               start=True, stop=True)
                    q.then_inc(s["q_ps"], 1)
                pe.wait_ge(s["nm_copied"], 1 + NT * b)
                for i in range(NT):
                    kv = mm(psX[:, 3 * D * i:3 * D * (i + 1)], xT[:, P * i:P * (i + 1)], wi[:, 2 * C:2 * C + 3 * D],
                            start=True, stop=True)
                kv.then_inc(s["kv_ps"], 1)
                pe.wait_ge(s["k_steps"], 1 + 9 * b + 9)
                for i in range(NT):
                    t = pe.transpose(psOb[0:ROW_MAX, P * i:P * (i + 1)],
                                     kp[:, i, :, :, :].rearrange("p a k d -> p (a k d)"), identb[:, :])
                t.then_inc(s["kT_ps"], 1)

            def max_piece(b, n):
                i, heads, lo, hi = PIECES[n]
                pe.wait_ge(s["m_max"], 1 + NPIECE * b + max(n - 1, 0))
                ps = psM[:, n % 2, 0:len(heads) * (hi - lo)].rearrange("p (h k) -> p h k", h=len(heads))
                diagonal = hi > P * i
                if diagonal:
                    mm(ps[:, :, hi - lo - P:hi - lo], identb[:, :],
                       tri[:, :].unsqueeze(1).to_broadcast([P, len(heads), P]), start=True, stop=False,
                       skip_group_check=True)
                for j, h in enumerate(heads):
                    m = mm(ps[:, j, :], QT[:, h, P * i:P * (i + 1)], KT[:, 0, lo:hi], start=not diagonal,
                           stop=True, skip_group_check=diagonal)
                m.then_inc(s["m_ps"], 1)

            def turn_max(b, i):
                pe.wait_ge(s["m_block"], 1 + NT * b + i + 1)
                pe.wait_ge(s["nm_copied"], 1 + NT * b + i)
                pe.transpose(psX[0:H, 0:P], nmx[:, i, :], ident[:, :]).then_inc(s["nmT_ps"], 1)

            def scores(b, n):
                i, kt = STEPS[n]
                if kt == 0:
                    pe.wait_ge(s[f"nm_rows{i % 2}"], 1 + 48 * (NT // 2 * b + i // 2 + 1))
                for u in range(2):
                    if n:
                        pe.wait_ge(s["exp_done"], 1 + 2 * (NSTEP * b + n) + u - 1)
                    for r in (2 * u, 2 * u + 1):
                        t0 = P * i + QC * r
                        v = 1 + r if kt == i else 0
                        m = mm(psS[:, r, :].rearrange("p (h t) -> p h t", h=H), KT[:, v, P * kt:P * (kt + 1)],
                               QT[:, :, t0:t0 + QC], start=True, stop=True)
                    m.then_inc(s["s_ps"], 1)

            def values(b, n):
                i, kt = STEPS[n]
                pe.wait_ge(s["exp_done"], 1 + 2 * (NSTEP * b + n) + 2)
                if kt == 0:
                    pe.wait_ge(s["o_evac"], 1 + NT * b + i)
                for r in range(4):
                    m = mm(psO[32 * r:32 * (r + 1), :], vx[:, kt, :], pT[:, n % PSLOTS, r, :],
                           start=(kt == 0), stop=(kt == i))
                m.then_inc(s["pv_done"], 1)

            def mp_stage(b):
                pe.wait_ge(s["q_rows"], 1 + N_Q * (b + 1))
                pe.wait_ge(s["kT_done"], 1 + NV * (b + 1))
                pe.wait_ge(s["v_done"], 1 + b + 1)
                pe.wait_ge(s["out_done"], 1 + b)
                pe.wait_ge(s["hs_done"], 1 + 2 * G * b)
                for what, n in ORDER:
                    {"M": max_piece, "T": turn_max, "S": scores, "V": values}[what](b, n)

            def o_stage(b, last):
                if not last:
                    pe.wait_ge(s["qb_done"], 1 + b + 2)
                    pe.wait_ge(s["qa_done"], 1 + b + 2)
                    pe.wait_ge(s["v_done"], 1 + b + 2)
                else:
                    pe.wait_ge(s["nm_copied"], 1 + NT * (b + 1))
                for c in range(2):
                    pe.wait_ge(s["a_done"], 1 + 2 * b + c + 1)
                    for j in range(4):
                        i = 4 * c + j
                        m = mm(psS[:, c, P * j:P * (j + 1)], aT[:, P * i:P * (i + 1)], wo[:, :], start=True, stop=True)
                    m.then_inc(s["pj_ps"], 1)
                for i in range(NT):
                    pe.wait_ge(s["xh2_done"], 1 + NT * b + i + 1)
                    t = pe.transpose(psS[:, 2 + i // 4, P * (i % 4):P * (i % 4 + 1)], xh2[:, i, :], ident[:, :])
                    if i % 4 == 3:
                        t.then_inc(s["x2T_ps"], 1)
                pe.wait_ge(s["x2T_act"], 1 + b + 1)
                pe.wait_ge(s["x2T_dve"], 1 + b + 1)
                for i in range(NT):
                    m = mm(psX[:, G * i:G * (i + 1)], x2T[:, P * i:P * (i + 1)], wr[:, :], start=True, stop=True)
                m.then_inc(s["rt_ps"], 1)

                def hidden(k):
                    c, e = divmod(k, G)
                    n = (G + 1) * c + e
                    if n == 0:
                        pe.wait_ge(s["y_done"], 1 + 2 * b + 2)
                    def free(m):
                        if m >= 4:
                            mc, me = divmod(m - 4, G + 1)
                            if me == G:
                                pe.wait_ge(s["shd_done"], 1 + 2 * b + mc + 1)
                            else:
                                pe.wait_ge(s["silu_done"], 1 + 2 * G * b + G * mc + me + 1)
                    xc = x2T[:, HALF * c:HALF * (c + 1)]
                    free(n)
                    if e < E:
                        m = mm(psS[:, n % 4, :], w1[:, e, :], xc, start=True, stop=True)
                    else:
                        mm(psS[:, n % 4, :], wgu[:, 0:C], xc, start=True, stop=True)
                        free(n + 1)
                        m = mm(psS[:, (n + 1) % 4, :], wgu[:, C:2 * C], xc, start=True, stop=True)
                    m.then_inc(s["h_ps"], 1)

                def expert_out(k):
                    c, e = divmod(k, G)
                    pe.wait_ge(s["hs_done"], 1 + 2 * G * b + k + 1)
                    for j in range(4):
                        m = mm(psM[:, c, P * j:P * (j + 1)], hs[:, k % 3, P * j:P * (j + 1)],
                               w2[:, e, :] if e < E else wsd[:, :],
                               start=(e == 0 and j == 0), stop=(e == E), skip_group_check=True)
                    m.then_inc(s["ye_ps"], 1)

                hidden(0)
                hidden(1)
                pe.wait_ge(s["cmb_done"], 1 + 2 * b + 2)
                pe.wait_ge(s["rt_steps"], 1 + 18 * b + 1)
                pe.transpose(psX[0:G * NT, 0:P], cmb[:, :, :].rearrange("p e i -> p (e i)"), ident[:, :]
                             ).then_inc(s["cT_ps"], 1)
                for k in range(2, 2 * G):
                    hidden(k)
                    expert_out(k - 2)
                expert_out(2 * G - 2)
                expert_out(2 * G - 1)

            pe.wait_ge(s["const_p"], 1 + NCP)
            pe.wait_ge(s["w_loaded"], 1 + NW)
            a_stage(0)
            with pe.Fori(0, B - 1) as b:
                mp_stage(b)
                a_stage(b + 1)
                o_stage(b, False)
            mp_stage(B - 1)
            o_stage(B - 1, True)

        @block.vector
        def _(dve):
            v = nc.vector
            v.memset(QT[:, :, :], 0.0).then_inc(s["const_v"], 1)
            v.memset(KT[:, :, :], 0.0).then_inc(s["const_v"], 1)
            v.memset(zrow[:, :], 0.0).then_inc(s["const_v"], 1)
            v.memset(vx[:, :, :], 0.0).then_inc(s["const_v"], 1)
            dve.wait_ge(s["const_v"], 1 + 4)
            v.memset(KT[64:ROW_MASK, :, :], 1.0).then_inc(s["const_v"], 1)
            v.memset(vx[:, :, D:2 * D], 1.0).then_inc(s["const_v"], 1)
            dve.wait_ge(s["const_v"], 1 + 6)

            def layer_stats(b, n, k, src, st, m_v, st_sem, mv_sem):
                base = NT * (n * b + k)
                for i in range(NT):
                    v.bn_stats(st[:, i, :], src(i)).then_inc(s[st_sem], 1)
                apart(dve, st_sem, base + NT)
                for i in range(NT):
                    v.bn_aggr(m_v[:, i, :], st[:, i, :]).then_inc(s[mv_sem], 1)

            def ln1(b):
                dve.wait_ge(s["x_loaded"], 1 + 16 * b + 16)
                layer_stats(b, 1, 0, lambda i: xt[:, i, :], stat, mv, "ln1_stat", "ln1_mv")

            def ln1_out(b):
                dve.wait_ge(s["ln1_rstd"], 1 + b + 1)
                dve.wait_ge(s["xT_ps"], 1 + 2 * b)
                for i in range(NT):
                    v.tensor_scalar(xh[:, i, :], xt[:, i, :], mv[:, i, 0:1], rstd[:, i:i + 1],
                                    ALU.subtract, ALU.mult).then_inc(s["ln1_out"], 1)

            def a_stage(b):
                dve.wait_ge(s["xT_ps"], 1 + 2 * b + 2)
                v.tensor_copy(xT[:, HALF:T], psS[:, 1, :]).then_inc(s["xT_dve"], 1)
                dve.wait_ge(s["q_ps"], 1 + 2 * b + 1)
                v.scalar_tensor_tensor(out=qa[:, :], in0=psS[:, 2:4, :].rearrange("p a t -> p (a t)"), scalar=bq[:, 0:1],
                                       in1=ropq[:, 0, :], op0=ALU.add, op1=ALU.mult).then_inc(s["qa_done"], 1)
                dve.wait_ge(s["q_ps"], 1 + 2 * b + 2)
                v.scalar_tensor_tensor(out=qb[:, :], in0=psS[:, 0:2, :].rearrange("p a t -> p (a t)"), scalar=bq[:, 1:2],
                                       in1=ropq[:, 1, :], op0=ALU.add, op1=ALU.mult).then_inc(s["qb_done"], 1)
                n = 5 * b
                dve.wait_ge(s["qa_done"], 1 + b + 1)
                dve.wait_ge(s["qb_done"], 1 + b + 1)
                v.tensor_tensor(qr[:, :], qa[:, :], qb[:, :], ALU.add).then_inc(s["q_steps"], 1)
                dve.wait_ge(s["q_steps"], 1 + n + 1)
                dve.wait_ge(s["q_scr_done"], 1 + 16 * b)
                v.tensor_copy(qp[:, 0, :], qr[:, :]).then_inc(s["q_steps"], 1)
                dve.wait_ge(s["q_steps"], 1 + n + 2)
                v.tensor_tensor(qa[:, :], qr[:, :], qp[:, 0, :], ALU.subtract).then_inc(s["q_steps"], 1)
                dve.wait_ge(s["q_steps"], 1 + n + 3)
                v.tensor_copy(qp[:, 1, :], qa[:, :]).then_inc(s["q_steps"], 1)
                dve.wait_ge(s["q_steps"], 1 + n + 4)
                v.tensor_tensor(qp[:, 2, :], qa[:, :], qp[:, 1, :], ALU.subtract).then_inc(s["q_steps"], 1)
                kv = psX[:, 0:3 * D * NT].rearrange("p (i w d) -> p w i d", w=3, d=D)
                n = 9 * b

                def bias(w):
                    return bkv[:, w, :].unsqueeze(1).to_broadcast([P, NT, D])

                dve.wait_ge(s["kv_ps"], 1 + b + 1)
                v.tensor_tensor(ka[:, :, :], kv[:, 0], bias(0), ALU.add).then_inc(s["k_steps"], 1)
                v.tensor_tensor(kb[:, :, :], kv[:, 1], bias(1), ALU.add).then_inc(s["k_steps"], 1)
                dve.wait_ge(s["pv_done"], 1 + NSTEP * b)
                v.tensor_tensor(vx[:, :, 0:D], kv[:, 2], bias(2), ALU.add).then_inc(s["v_done"], 1)
                dve.wait_ge(s["k_steps"], 1 + n + 2)
                v.tensor_tensor(ka[:, :, :], ka[:, :, :], ropk[:, 0], ALU.mult).then_inc(s["k_steps"], 1)
                v.tensor_tensor(kb[:, :, :], kb[:, :, :], ropk[:, 1], ALU.mult).then_inc(s["k_steps"], 1)
                dve.wait_ge(s["k_steps"], 1 + n + 4)
                v.tensor_tensor(kr[:, :, :], ka[:, :, :], kb[:, :, :], ALU.add).then_inc(s["k_steps"], 1)
                dve.wait_ge(s["k_steps"], 1 + n + 5)

                def part(k):
                    return kp[:, :, :, k, :]

                def thrice(t):
                    return t[:, :, :].unsqueeze(2).to_broadcast([P, NT, PARTS, D])

                v.tensor_copy(part(0), thrice(kr)).then_inc(s["k_steps"], 1)
                dve.wait_ge(s["k_steps"], 1 + n + 6)
                v.tensor_tensor(ka[:, :, :], kr[:, :, :], kp[:, :, 0, 0, :], ALU.subtract).then_inc(s["k_steps"], 1)
                dve.wait_ge(s["k_steps"], 1 + n + 7)
                v.tensor_copy(part(1), thrice(ka)).then_inc(s["k_steps"], 1)
                dve.wait_ge(s["k_steps"], 1 + n + 8)
                v.tensor_tensor(part(2), thrice(ka), part(1), ALU.subtract).then_inc(s["k_steps"], 1)
                dve.wait_ge(s["kT_ps"], 1 + b + 1)
                v.tensor_copy(KT[0:ROW_MAX, 0, :], psOb[0:ROW_MAX, :]).then_inc(s["kT_done"], 1)
                dve.wait_ge(s["kT_done"], 1 + NV * b + 1)
                for w in range(1, NV):
                    v.tensor_copy(KT[0:ROW_MAX, w, :], KT[0:ROW_MAX, 0, :]).then_inc(s["kT_done"], 1)

            def max_piece(b, n):
                i, heads, lo, hi = PIECES[n]
                dve.wait_ge(s["m_ps"], 1 + NPIECE * b + n + 1)
                cut = nmx[:, i, :] if i < BT else nmx2[:, i - BT, lo // BANK, :]
                v.tensor_reduce(cut[:, heads[0]:heads[-1] + 1],
                                psM[:, n % 2, 0:len(heads) * (hi - lo)].rearrange("p (h k) -> p h k", h=len(heads)),
                                AX.X, ALU.max, negate=True).then_inc(s["m_max"], 1)
                if n + 1 == NPIECE or PIECES[n + 1][0] > i:
                    dve.wait_ge(s["m_max"], 1 + NPIECE * b + n + 1)
                    if i < BT:
                        dve.sem_inc(s["m_block"], 1)
                    else:
                        v.tensor_tensor(nmx[:, i, :], nmx2[:, i - BT, 0, :], nmx2[:, i - BT, 1, :],
                                        ALU.min).then_inc(s["m_block"], 1)

            def copy_max(b, i):
                dve.wait_ge(s["nmT_ps"], 1 + NT * b + i + 1)
                if i >= 2:
                    dve.wait_ge(s["nm_steps"], 1 + 4 * (NT * b + i - 1))
                else:
                    dve.wait_ge(s["nm_steps"], 1 + 4 * NT * b)
                v.tensor_copy(nm[:, i % 2, :], psX[0:H, 0:P]).then_inc(s["nm_copied"], 1)

            def evacuate(b, i):
                dve.wait_ge(s["pv_done"], 1 + NSTEP * b + STEPS.index((i, i)) + 1)
                dve.wait_ge(s[f"o_written{i % 2}"], 1 + N_O * b + 128 * (i // 2))
                v.tensor_copy(osb[:, i % 2, :], psO[:, :]).then_inc(s["o_evac"], 1)

            def mp_stage(b, last):
                for what, n in ORDER:
                    if what == "M":
                        max_piece(b, n)
                    elif what == "T":
                        copy_max(b, n)
                    elif what == "V":
                        i, kt = STEPS[n]
                        if kt == i:
                            evacuate(b, i)
                        if not last and (i, kt) == (6, 0):
                            ln1(b + 1)
                        if not last and (i, kt) == (7, 0):
                            ln1_out(b + 1)

            def o_stage(b, last):
                for c in range(2):
                    h = slice(HALF * c, HALF * (c + 1))
                    dve.wait_ge(s[f"o_read{c}"], 1 + 32 * b + 32)
                    v.reciprocal(rD[:, h], dT[:, h]).then_inc(s["den_inv"], 1)
                    dve.wait_ge(s["den_inv"], 1 + 2 * b + c + 1)
                    v.tensor_tensor(aT[:, h], oT[:, h], rD[:, h], ALU.mult).then_inc(s["a_done"], 1)
                dve.wait_ge(s["stored"], 1 + 16 * b)
                for c in range(2):
                    dve.wait_ge(s["pj_ps"], 1 + 2 * b + c + 1)
                    v.tensor_tensor(y[:, 4 * c:4 * c + 4, :], psS[:, c, :].rearrange("p (i n) -> p i n", n=C),
                                    bo[:, :].unsqueeze(1).to_broadcast([P, 4, C]), ALU.add).then_inc(s["y_done"], 1)
                dve.wait_ge(s["y_done"], 1 + 2 * b + 2)
                layer_stats(b, 3, 0, lambda i: y[:, i, :], ostat, omv, "lnO_stat", "lnO_mv")
                dve.wait_ge(s["lnO_rstd"], 1 + 3 * b + 1)
                for i in range(NT):
                    v.tensor_scalar(y[:, i, :], y[:, i, :], omv[:, i, 0:1], orstd[:, i:i + 1],
                                    ALU.subtract, ALU.mult).then_inc(s["yn_done"], 1)
                dve.wait_ge(s["xr_loaded"], 1 + 16 * b + 16)
                dve.wait_ge(s["yn_done"], 1 + NT * (2 * b + 1))
                v.tensor_tensor(x1[:, :, :], xr[:, :, :], y[:, :, :], ALU.add).then_inc(s["x1_done"], 1)
                dve.wait_ge(s["x1_done"], 1 + b + 1)
                layer_stats(b, 3, 1, lambda i: x1[:, i, :], ostat, omv, "lnO_stat", "lnO_mv")
                dve.wait_ge(s["lnO_rstd"], 1 + 3 * b + 2)
                for i in range(NT):
                    v.tensor_scalar(xh2[:, i, :], x1[:, i, :], omv[:, i, 0:1], orstd[:, i:i + 1],
                                    ALU.subtract, ALU.mult).then_inc(s["xh2_done"], 1)
                dve.wait_ge(s["x2T_ps"], 1 + 2 * b + 2)
                v.tensor_copy(x2T[:, HALF:T], psS[:, 3, :]).then_inc(s["x2T_dve"], 1)
                router(b)
                for c in range(2):
                    for e in range(G):
                        k = G * c + e
                        dve.wait_ge(s["silu_done"], 1 + 2 * G * b + k + 1)
                        src = hsil[:, k % 3, :]
                        if e == E:
                            v.tensor_tensor(shd[:, :], psS[:, ((G + 1) * c + G) % 4, :], src, ALU.mult).then_inc(s["shd_done"], 1)
                            dve.wait_ge(s["shd_done"], 1 + 2 * b + c + 1)
                            src = shd[:, :]
                        dve.wait_ge(s["cb_done"], 1 + 2 * G * b + k + 1)
                        if k >= 3:
                            dve.wait_ge(s["ye_ps"], 1 + 2 * G * b + k - 2)
                        else:
                            dve.wait_ge(s["ye_ps"], 1 + 2 * G * b)
                        v.tensor_tensor(hs[:, k % 3, :], src, cb[:, k % 3, :], ALU.mult).then_inc(s["hs_done"], 1)
                dve.wait_ge(s["ye_ps"], 1 + 2 * G * (b + 1))
                ye = psM[:, :, :].rearrange("p c (j n) -> p (c j) n", n=C)
                layer_stats(b, 3, 2, lambda i: ye[:, i, :], ostat, omv, "lnO_stat", "lnO_mv")
                dve.wait_ge(s["lnO_rstd"], 1 + 3 * b + 3)
                for i in range(NT):
                    v.tensor_scalar(y[:, i, :], ye[:, i, :], omv[:, i, 0:1], orstd[:, i:i + 1],
                                    ALU.subtract, ALU.mult).then_inc(s["yn_done"], 1)
                dve.wait_ge(s["yn_done"], 1 + NT * (2 * b + 2))
                v.tensor_tensor(y[:, :, :], y[:, :, :], x1[:, :, :], ALU.add).then_inc(s["out_done"], 1)

            def router(b):
                n = 18 * b
                step = [0]

                def then(ins):
                    ins.then_inc(s["rt_steps"], 1)
                    step[0] += 1
                    dve.wait_ge(s["rt_steps"], 1 + n + step[0])

                def wide(t):
                    return t[:, :, :].to_broadcast([P, NT, E])

                dve.wait_ge(s["rt_ps"], 1 + b + 1)
                then(v.tensor_copy(lg[:, :, :], psX[:, 0:G * NT].rearrange("p (i e) -> p i e", e=G)))
                then(v.tensor_reduce(red[:, :, 0], lg[:, :, 0:E], AX.X, ALU.max))
                v.tensor_tensor(ls[:, :, :], lg[:, :, 0:E], wide(red), ALU.subtract).then_inc(s["ls_done"], 1)
                dve.wait_ge(s["ex_done"], 1 + 2 * b + 2)
                then(v.tensor_reduce(red[:, :, 0], ex[:, :, :], AX.X, ALU.add))
                then(v.reciprocal(red[:, :, :], red[:, :, :]))
                then(v.tensor_tensor(pr[:, :, :], ex[:, :, :], wide(red), ALU.mult))
                then(v.tensor_reduce(red[:, :, 0], pr[:, :, :], AX.X, ALU.max))
                then(v.tensor_tensor(eq[:, :, :], pr[:, :, :], wide(red), ALU.is_equal))
                then(v.tensor_tensor(cand[:, :, :], eq[:, :, :], rank[:, :, :], ALU.mult))
                then(v.tensor_reduce(red[:, :, 0], cand[:, :, :], AX.X, ALU.max))
                then(v.tensor_tensor(oh1[:, :, :], cand[:, :, :], wide(red), ALU.is_equal))
                then(v.scalar_tensor_tensor(out=p2[:, :, :], in0=oh1[:, :, :], scalar=-2.0, in1=pr[:, :, :],
                                            op0=ALU.mult, op1=ALU.add))
                then(v.tensor_reduce(red[:, :, 0], p2[:, :, :], AX.X, ALU.max))
                then(v.tensor_tensor(eq[:, :, :], p2[:, :, :], wide(red), ALU.is_equal))
                then(v.tensor_tensor(cand[:, :, :], eq[:, :, :], rank[:, :, :], ALU.mult))
                then(v.tensor_reduce(red[:, :, 0], cand[:, :, :], AX.X, ALU.max))
                then(v.tensor_tensor(oh2[:, :, :], cand[:, :, :], wide(red), ALU.is_equal))
                then(v.tensor_tensor(oh1[:, :, :], oh1[:, :, :], oh2[:, :, :], ALU.add))
                then(v.tensor_scalar(eg[:, :], eg[:, :], 1.0, None, ALU.add))
                assert step[0] == 18
                v.reciprocal(cmb[:, E, :], eg[:, :]).then_inc(s["cmb_done"], 1)
                v.tensor_tensor(cmb[:, 0:E, :].rearrange("p e i -> p i e"), pr[:, :, :], oh1[:, :, :],
                                ALU.mult).then_inc(s["cmb_done"], 1)
                dve.wait_ge(s["cT_ps"], 1 + b + 1)
                dve.wait_ge(s["crow_done"], 1 + G * 16 * b)
                v.tensor_copy(cT[:, :], psX[0:G * NT, 0:P]).then_inc(s["cT_done"], 1)

            ln1(0)
            ln1_out(0)
            dve.wait_ge(s["w_loaded"], 1 + NW)
            a_stage(0)
            with dve.Fori(0, B - 1) as b:
                mp_stage(b, False)
                a_stage(b + 1)
                o_stage(b, False)
            mp_stage(B - 1, True)
            o_stage(B - 1, True)


def rope_tables():
    pos = np.arange(T, dtype=np.float32)
    freqs = (np.float32(1.0) / np.float32(10000.0) ** (np.arange(0, D, 2, dtype=np.float32) / np.float32(D))).astype(np.float32)
    ang = (pos[:, None] * freqs[None, :]).astype(np.float32)
    sin, cos = np.sin(ang), np.cos(ang)
    c = np.concatenate([cos, -cos], 1)
    n = np.concatenate([sin, sin], 1)
    q = np.stack([np.tile(c.T, (H, 1)), np.tile(n.T, (H, 1))], 1)
    k = np.stack([c.reshape(NT, P, D).transpose(1, 0, 2), n.reshape(NT, P, D).transpose(1, 0, 2)], 1)
    return np.ascontiguousarray(q, np.float32), np.ascontiguousarray(k, np.float32)


def kernel(L0_attn_x, L0_attn_Wq, L0_attn_bq, L0_attn_Wk, L0_attn_bk, L0_attn_Wv, L0_attn_bv, L0_attn_Wo, L0_attn_bo,
           L0_ffn_router_w, L0_ffn_w1, L0_ffn_w2, L0_ffn_shared_gate_up, L0_ffn_shared_down, L0_ffn_shared_gate_w):
    import concourse.bacc as bacc
    from concourse.bass_utils import run_bass_kernel_spmd

    def swap(w):
        w = np.asarray(w)
        return w.reshape(*w.shape[:-1], -1, 2, D // 2)[..., ::-1, :].reshape(w.shape)

    rope_q, rope_k = rope_tables()
    bkv = np.concatenate([np.asarray(L0_attn_bk), swap(L0_attn_bk), np.asarray(L0_attn_bv)]).reshape(1, 3, D)
    arrays = {
        "x": L0_attn_x,
        "w_in": np.concatenate([L0_attn_Wq, swap(L0_attn_Wq), L0_attn_Wk, swap(L0_attn_Wk), L0_attn_Wv], 1),
        "w_out": L0_attn_Wo,
        "b_q": np.stack([np.asarray(L0_attn_bq), swap(L0_attn_bq)], 1),
        "b_kv": np.broadcast_to(bkv, (P, 3, D)),
        "b_o": np.broadcast_to(np.asarray(L0_attn_bo)[None], (P, C)),
        "rope_q": rope_q,
        "rope_k": rope_k,
        "w_router": np.concatenate([L0_ffn_router_w, L0_ffn_shared_gate_w], 1),
        "w_up": L0_ffn_w1,
        "w_down": L0_ffn_w2,
        "w_gu": L0_ffn_shared_gate_up,
        "w_sd": L0_ffn_shared_down,
    }
    arrays = {n: np.ascontiguousarray(a) for n, a in arrays.items()}
    nc = bacc.Bacc("TRN2", target_bir_lowering=False, num_devices=1)
    args = [nc.dram_tensor(n, a.shape, F32, kind="ExternalInput").ap() for n, a in arrays.items()]
    out = nc.dram_tensor("out", (B, T, C), F32, kind="ExternalOutput").ap()
    build(nc, *args, out)
    r = run_bass_kernel_spmd(nc, [arrays], core_ids=[0])
    return r.results[0]["out"]
```

```python
from contextlib import ExitStack

import numpy as np

import concourse.bass as bass
from concourse import mybir

F32 = mybir.dt.float32
BF16 = mybir.dt.bfloat16
ALU = mybir.AluOpType
ACT = mybir.ActivationFunctionType
AX = mybir.AxisListType

P = 128
B, T, C = 4, 1024, 128
H, D = 16, 8
E = 8
G = E + 1
NT = T // P
QC = 32
NR = P // QC
NV = 1 + NR
BANK = 512
BT = BANK // P
HALF = T // 2
HT = HALF // P
PARTS = 3
ROW_MAX = PARTS * PARTS * D
ROW_MASK = 96
MASKED = -1e30
EPS = 1e-5
VW = 32
SLOTS = 3
EARLY = 4


def maximum_pieces():
    pieces = []
    for i in range(NT):
        lo, hi = BANK * (i // BT), P * (i + 1)
        if lo:
            pieces += [(i, [h], 0, lo) for h in range(H)]
        n = BANK // (hi - lo)
        pieces += [(i, list(range(h, h + n)), lo, hi) for h in range(0, H, n)]
    return pieces


PIECES = maximum_pieces()
NPIECE = len(PIECES)
OF_TILE = [[n for n, p in enumerate(PIECES) if p[0] == i] for i in range(NT)]
STEPS = [(i, kt) for i in range(NT) for kt in range(i + 1)]
NSTEP = len(STEPS)
NQ = NR * NSTEP

USES_X = ("T", "a_turn", "a_q", "a_qs", "a_kv", "a_kT", "o_proj", "o_turn", "o_rt", "o_cT")


def spread(items, start, end):
    return [(start + (end - start) * (k + 0.5) / len(items), it) for k, it in enumerate(items)]


def a_items(d, c, at):
    return [(at + x, (name, d, c)) for x, name in (
        (0.0, "a_stat"), (0.7, "a_norm"), (1.0, "a_turn"), (1.3, "a_q"), (1.6, "a_qs"), (2.0, "a_split"),
        (2.0, "a_kv"), (3.0, "a_kT"))]


def o_items(d, c, at, pace=0.8):
    items = [(at + x, (name, d, c)) for x, name in (
        (-0.5, "o_load"), (0.0, "o_div"), (1.5, "o_aT"), (1.6, "o_proj"), (1.9, "o_st2"), (2.5, "o_n2"), (3.0, "o_st3"),
        (3.5, "o_n3"), (3.7, "o_turn"), (4.0, "o_rt"), (4.3, "o_top"), (4.8, "o_cT"))]
    h0 = at + 5.3
    items += [(h0 + pace * e, ("o_h", d, (c, e))) for e in range(G)]
    items += [(h0 + pace * (E + 1), ("o_up", d, c))]
    items += [(h0 + pace * (e + 1.7 + (e == E)), ("o_y", d, (c, e))) for e in range(G)]
    last = h0 + pace * (E + 3)
    return items + [(last + 0.2, ("o_st4", d, c)), (last + 0.8, ("o_n4", d, c))]


def order_of(placed):
    return [it for _, it in sorted(placed, key=lambda p: p[0])]


def early_maximum(d, start, end):
    placed = spread([("M", d, n) for i in range(EARLY) for n in OF_TILE[i]], start, end)
    for i in range(EARLY):
        after = max(x for x, it in placed if it[0] == "M" and it[2] == OF_TILE[i][-1])
        placed.append((after + 0.35, ("T", d, i)))
    return placed


def body_order(first, last):
    placed = [(-1.0, ("keys", 0, 0)), (-1.0, ("a_rows", 0, 1))]
    for n, (i, kt) in enumerate(STEPS):
        placed += [(n + 0.2 * r, ("S", 0, (n, r))) for r in range(NR)]
        placed += [(n + 1.1, ("V", 0, n))]
        if kt == i:
            placed += [(n + 1.15, ("evac", 0, i))]
            if i % HT == HT - 1:
                placed += [(n + 1.2, ("o_read", 0, i // HT))]
    begin = -0.5
    for i in range(EARLY, NT):
        end = i * (i + 1) / 2 - 2.2
        placed += spread([("M", 0, n) for n in OF_TILE[i]], begin, end)
        placed += [(end + 0.35, ("T", 0, i))]
        begin = end
    if not first:
        placed += o_items(-1, 1, 1.0)
    placed += o_items(0, 0, 16.0)
    if not last:
        placed += [(-0.9, ("a_load", 1, 0)), (-0.9, ("a_load", 1, 1))]
        placed += a_items(1, 0, 8.0) + [(13.0, ("a_rows", 1, 0))] + a_items(1, 1, 14.0)
        placed += early_maximum(1, begin + 0.1, NSTEP - 0.7)
    return order_of(placed)


PROLOGUE = ([("a_load", 0, 0), ("a_load", 0, 1)] + order_of(a_items(0, 0, 0.0)) + [("a_rows", 0, 0)]
            + order_of(a_items(0, 1, 0.0)) + order_of(early_maximum(0, 0.0, 8.0)))
FIRST, BODY, LAST = body_order(True, False), body_order(False, False), body_order(False, True)
TAIL = order_of(o_items(0, 1, 0.0))


def uses_x(order):
    return sum(it[0] in USES_X for it in order)


def build(nc, x, w_in, w_out, b_q, b_kv, b_o, rope_q, rope_k, w_router, w_up, w_down, w_gu, w_sd, out):
    with ExitStack() as ctx:
        def sb(name, shape, dt=F32):
            return ctx.enter_context(nc.sbuf_tensor(name, shape, dt))

        def pb(name, shape, dt=F32):
            return ctx.enter_context(nc.psum_tensor(name, shape, dt))

        q_scr = nc.dram_tensor("q_scr", (2, PARTS, P, HALF), BF16, kind="Internal").ap()
        num_scr = nc.dram_tensor("num_scr", (2, P, HALF), F32, kind="Internal").ap()
        den_scr = nc.dram_tensor("den_scr", (2, H, HALF), F32, kind="Internal").ap()
        inv_scr = nc.dram_tensor("inv_scr", (2, H, HALF), F32, kind="Internal").ap()

        wi = sb("wi", [P, 2 * C + 3 * D])
        wo = sb("wo", [P, C])
        bq = sb("bq", [P, 2])
        bkv = sb("bkv", [P, 3, D])
        bo = sb("bo", [P, C])
        ropq = sb("ropq", [P, 2, T])
        ropk = sb("ropk", [P, 2, NT, D])
        wr = sb("wr", [P, G])
        w1 = sb("w1", [P, E, C])
        w2 = sb("w2", [P, E, C])
        wgu = sb("wgu", [P, 2 * C])
        wsd = sb("wsd", [P, C])
        tri = sb("tri", [P, P], BF16)
        ident = sb("ident", [P, P])
        identb = sb("identb", [P, P], BF16)
        half_pow = sb("half_pow", [P, HT])
        rank = sb("rank", [P, HT, E])
        zrow = sb("zrow", [P, HALF], BF16)

        xt = sb("xt", [P, 2, HT, C])
        xh = sb("xh", [P, 2, HT, C])
        xT = sb("xT", [P, 2, HALF])
        stat = sb("stat", [P, HT, 6])
        mv = sb("mv", [P, 2, HT, 2])
        veps = sb("veps", [P, HT])
        rstd = sb("rstd", [P, 2, HT])
        qa = sb("qa", [P, HALF])
        qb = sb("qb", [P, HALF])
        qr = sb("qr", [P, HALF])
        qp = sb("qp", [P, 2, PARTS, HALF], BF16)
        ka = sb("ka", [P, HT, D])
        kb = sb("kb", [P, HT, D])
        kr = sb("kr", [P, HT, D])
        kp = sb("kp", [P, HT, PARTS, PARTS, D], BF16)
        QT = sb("QT", [P, H, T], BF16)
        KT = sb("KT", [P, NV, T], BF16)
        KN = sb("KN", [P, T], BF16)
        vx = sb("vx", [P, NT, VW])
        vn = sb("vn", [P, NT, D])
        nmx = sb("nmx", [P, NT, H])
        nmx2 = sb("nmx2", [P, NT // 2, 2, H])
        nm = sb("nm", [H, 2, P])
        nmr = sb("nmr", [H, 2, P])
        nmp = sb("nmp", [H, 2, PARTS, P], BF16)
        pT = sb("pT", [P, SLOTS, NR, BANK])
        osb = sb("osb", [P, 2, BANK])
        oT = sb("oT", [P, 2, HALF])
        dn = sb("dn", [P, H * HALF // P])
        di = sb("di", [P, H * HALF // P])
        dT = sb("dT", [P, HALF])
        aT = sb("aT", [P, HALF])
        xr = sb("xr", [P, 2, HT, C])
        y = sb("y", [P, 2, HT, C])
        x1 = sb("x1", [P, 2, HT, C])
        xh2 = sb("xh2", [P, HT, C])
        x2T = sb("x2T", [P, 2, HALF])
        ostat = sb("ostat", [P, HT, 6])
        omv = sb("omv", [P, HT, 2])
        oveps = sb("oveps", [P, HT])
        orstd = sb("orstd", [P, HT])
        lg = sb("lg", [P, HT, G])
        ls = sb("ls", [P, HT, E])
        ex = sb("ex", [P, HT, E])
        eg = sb("eg", [P, HT])
        pr = sb("pr", [P, HT, E])
        p2 = sb("p2", [P, HT, E])
        eq = sb("eq", [P, HT, E])
        cand = sb("cand", [P, HT, E])
        oh1 = sb("oh1", [P, HT, E])
        oh2 = sb("oh2", [P, HT, E])
        red = sb("red", [P, HT, 1])
        cmb = sb("cmb", [P, G, HT])
        cT = sb("cT", [G * HT, P])
        crow = sb("crow", [P, 2, 3, HALF])
        cb = sb("cb", [P, SLOTS, BANK])
        th = sb("th", [P, SLOTS, BANK])
        hg = sb("hg", [P, SLOTS, BANK])
        hs = sb("hs", [P, SLOTS, BANK])
        shd = sb("shd", [P, BANK])

        psS = pb("psS", [P, 2, BANK])
        psM = pb("psM", [P, 2, BANK])
        psO = pb("psO", [P, BANK])
        psX = pb("psX", [P, BANK])
        psH = pb("psH", [P, BANK])
        psY = pb("psY", [P, BANK])
        psXb = psX[:, :].bitcast(BF16)

        s = {n: ctx.enter_context(nc.semaphore(n)) for n in (
            "w_loaded", "const_v", "const_p", "x_loaded0", "x_loaded1", "xr_loaded0", "xr_loaded1",
            "x_written", "x_read",
            "a_stat", "a_mv", "a_veps", "a_rstd", "xh_done", "q_sum", "q_hi", "q_rest", "q_mid", "q_lo",
            "qa_done", "qb_done", "q_sent", "q_rows0", "q_rows1", "k_steps", "vn_done", "kp_done", "KN_done", "KT_done", "vx_done",
            "m_ps", "m_max", "m_block", "nm_copied", "nm_steps", "nm_rows0", "nm_rows1",
            "s_ps", "exp_done", "pv_done", "o_evac", "o_written0", "o_written1", "num_read", "den_read",
            "den_inv", "inv_written", "inv_read", "aT_done",
            "y_done", "o_stat", "o_mv", "o_veps", "o_rstd", "yn_done", "x1_done", "xh2_done", "x2T_done",
            "rt_steps", "ls_done", "ex_done", "cmb_done", "cT_done",
            "crow_done", "cb_done", "h_written", "h_read", "th_done", "sg_done", "hg_done", "hs_done", "ye_ps",
            "out_done", "stored0", "stored1", "passed", "vx_ones")}

        names = list(s)
        with nc.Block() as start:
            for n, on in enumerate((start.sync, start.scalar, start.tensor, start.vector, start.gpsimd)):
                @on
                def _(eng, n=n):
                    for name in names[n::5]:
                        eng.sem_inc(s[name], 1)

        def after(count):
            return 1 + (max(count, 0) if isinstance(count, int) else count)


        def follow(eng, items):
            def run(order, b, used):
                for name, d, what in order:
                    if name in items:
                        items[name](b + d, what, used)
                    if name in USES_X:
                        used = used + 1

            n0, n1, n2, n3 = (uses_x(o) for o in (PROLOGUE, FIRST, BODY, LAST))
            run(PROLOGUE, 0, 0)
            run(FIRST, 0, n0)
            with eng.Fori(1, B - 1) as b:
                run(BODY, b, n0 + n1 - n2 + n2 * b)
            run(LAST, B - 1, n0 + n1 + n2 * (B - 2))
            run(TAIL, B - 1, n0 + n1 + n2 * (B - 2) + n3)

        xb = x.rearrange("b (c i p) n -> b c p i n", p=P, c=2)
        ob = out.rearrange("b (c i p) n -> b c p i n", p=P, c=2)
        N_OW = NT // 2 * 8 * 16
        NW = 12 * 16
        NCV = 7
        NCP = 8 + NR + 1

        block = ctx.enter_context(nc.Block())

        @block.sync
        def _(sp):
            def a_load(b, c, used):
                sp.wait_ge(s["xh_done"], after(HT * (2 * b + c - 1)))
                sp.sem_inc(s["passed"], 1)
                sp.dma_start(xt[:, c, :, :], xb[b, c]).then_inc(s[f"x_loaded{c}"], 16)

            def a_rows(b, c, used):
                u = 2 * b + c
                sp.wait_ge(s["q_lo"], after(u + 1))
                sp.dma_start(q_scr[c].rearrange("a p t -> p a t"), qp[:, c, :, :]).then_inc(s["q_sent"], 16)
                sp.wait_ge(s["s_ps"], after(NQ * (b - 1) + NR * (NSTEP if c else EARLY * (EARLY + 1) // 2)))
                t = slice(HALF * c, HALF * (c + 1))
                sp.dma_start(QT[ROW_MAX:ROW_MAX + PARTS, :, t],
                             zrow[0:PARTS, :].unsqueeze(1).to_broadcast([PARTS, H, HALF])).then_inc(s[f"q_rows{c}"], 16)
                sp.wait_ge(s["q_sent"], after(16 * (u + 1)))
                for a in range(PARTS):
                    for k in range(PARTS):
                        r = (PARTS * a + k) * D
                        sp.dma_start(QT[r:r + D, :, t],
                                     q_scr[c, a].rearrange("(h j) t -> j h t", j=D)).then_inc(s[f"q_rows{c}"], 16)

            def turn_max(b, i, used):
                sp.wait_ge(s["nm_steps"], after(4 * (NT * b + i) + 4))
                for a in range(PARTS):
                    sp.dma_start(QT[ROW_MAX + a:ROW_MAX + a + 1, :, P * i:P * (i + 1)],
                                 nmp[:, i % 2, a, :]).then_inc(s[f"nm_rows{i % 2}"], 16)

            def evac(b, i, used):
                sp.wait_ge(s["o_evac"], after(NT * b + i + 1))
                c = i // HT
                for r in range(NR):
                    t = slice(P * (i % HT) + QC * r, P * (i % HT) + QC * (r + 1))
                    sp.dma_start(num_scr[c].rearrange("(h d) t -> d h t", d=D)[:, :, t],
                                 osb[32 * r:32 * r + D, i % 2, :].rearrange("d (h t) -> d h t", h=H)
                                 ).then_inc(s[f"o_written{i % 2}"], 16)
                    sp.dma_start(den_scr[c][:, t].unsqueeze(0),
                                 osb[32 * r + D:32 * r + D + 1, i % 2, :].rearrange("d (h t) -> d h t", h=H)
                                 ).then_inc(s[f"o_written{i % 2}"], 16)

            def o_read(b, c, used):
                u = 2 * b + c
                for w in range(2):
                    sp.wait_ge(s[f"o_written{w}"], after(N_OW * b + (N_OW // 2) * (c + 1)))
                    sp.sem_inc(s["passed"], 1)
                sp.wait_ge(s["aT_done"], after(u - 1))
                sp.dma_start(oT[:, c, :], num_scr[c]).then_inc(s["num_read"], 16)
                sp.wait_ge(s["den_inv"], after(u))
                sp.dma_start(dn[:, :], den_scr[c].rearrange("h (x t) -> (h x) t", x=P // H)).then_inc(s["den_read"], 16)

            def o_div(b, c, used):
                u = 2 * b + c
                sp.wait_ge(s["den_inv"], after(u + 1))
                sp.dma_start(inv_scr[c].rearrange("h (x t) -> (h x) t", x=P // H), di[:, :]).then_inc(s["inv_written"], 16)
                sp.wait_ge(s["inv_written"], after(16 * (u + 1)))
                sp.sem_inc(s["passed"], 1)
                sp.wait_ge(s["aT_done"], after(u))
                sp.dma_start(dT[:, :], inv_scr[c].unsqueeze(1).to_broadcast([H, D, HALF])).then_inc(s["inv_read"], 16)

            def o_load(b, c, used):
                sp.wait_ge(s["x1_done"], after(2 * b + c - 1))
                sp.sem_inc(s["passed"], 1)
                sp.dma_start(xr[:, c, :, :], xb[b, c]).then_inc(s[f"xr_loaded{c}"], 16)

            def o_cT(b, c, used):
                u = 2 * b + c
                sp.wait_ge(s["cT_done"], after(u + 1))
                sp.sem_inc(s["passed"], 1)
                sp.wait_ge(s["cb_done"], after(G * (u - 1)))
                for e in range(G):
                    sp.dma_start(crow[32 * (e % 4):32 * (e % 4) + 1, c, e // 4, :].rearrange("o (i t) -> o i t", t=P),
                                 cT[HT * e:HT * (e + 1), :]).then_inc(s["crow_done"], 16)

            def o_n4(b, c, used):
                sp.wait_ge(s["out_done"], after(2 * b + c + 1))
                sp.sem_inc(s["passed"], 1)
                sp.dma_start(ob[b, c], y[:, c, :, :]).then_inc(s[f"stored{c}"], 16)

            for dst, src in [(wi[:, :], w_in), (ropq[:, :, :], rope_q), (ropk[:, :, :, :], rope_k),
                             (bq[:, :], b_q), (bkv[:, :, :], b_kv), (bo[:, :], b_o), (wo[:, :], w_out), (wr[:, :], w_router),
                             (w1[:, :, :], w_up.rearrange("e d f -> d e f")), (w2[:, :, :], w_down.rearrange("e f d -> f e d")),
                             (wgu[:, :], w_gu), (wsd[:, :], w_sd)]:
                sp.dma_start(dst, src).then_inc(s["w_loaded"], 16)
            sp.wait_ge(s["const_v"], after(NCV))
            follow(sp, {"a_load": a_load, "a_rows": a_rows, "T": turn_max, "evac": evac, "o_read": o_read,
                        "o_div": o_div, "o_load": o_load, "o_cT": o_cT, "o_n4": o_n4})
            for c in range(2):
                sp.wait_ge(s[f"stored{c}"], after(16 * B))

        @block.gpsimd
        def _(pool):
            pool.memset(ident[:, :], 0.0).then_inc(s["const_p"], 1)
            pool.memset(identb[:, :], 0.0).then_inc(s["const_p"], 1)
            pool.memset(tri[:, :], 0.0).then_inc(s["const_p"], 1)
            pool.memset(half_pow[:, :], -0.5).then_inc(s["const_p"], 1)
            pool.wait_ge(s["const_p"], after(4))
            pool.affine_select(out=ident[:, :], in_=ident[:, :], compare_op=ALU.not_equal, fill=1.0,
                               base=0, pattern=[[-1, P]], channel_multiplier=1).then_inc(s["const_p"], 1)
            pool.affine_select(out=identb[:, :], in_=identb[:, :], compare_op=ALU.not_equal, fill=1.0,
                               base=0, pattern=[[-1, P]], channel_multiplier=1).then_inc(s["const_p"], 1)
            pool.affine_select(out=tri[:, :], in_=tri[:, :], compare_op=ALU.is_ge, fill=MASKED,
                               base=0, pattern=[[-1, P]], channel_multiplier=1).then_inc(s["const_p"], 1)
            pool.iota(rank[:, :, :], pattern=[[0, HT], [-1, E]], base=E, channel_multiplier=0,
                      allow_small_or_imprecise_dtypes=True).then_inc(s["const_p"], 1)
            pool.wait_ge(s["const_p"], after(8))
            pool.wait_ge(s["const_v"], after(NCV))
            m = QT[ROW_MASK:P, :, :].rearrange("p h (c t) -> p (h c) t", t=QC)
            pool.affine_select(out=m, in_=m, compare_op=ALU.not_equal, fill=1.0, base=0,
                               pattern=[[0, H * T // QC], [1, QC]], channel_multiplier=-1).then_inc(s["const_p"], 1)
            for v in range(1, NV):
                pool.wait_ge(s["const_p"], after(8 + v))
                m = KT[ROW_MASK:P, v, :].rearrange("p (i k) -> p i k", k=P)
                pool.affine_select(out=m, in_=m, compare_op=ALU.is_ge, fill=MASKED, base=QC * (v - 1),
                                   pattern=[[0, NT], [-1, P]], channel_multiplier=1).then_inc(s["const_p"], 1)
            pool.wait_ge(s["const_p"], after(NCP))

            def rstd_of(n, var, ve, rs, mv_sem, ve_sem, rs_sem):
                pool.wait_ge(s[mv_sem], after(HT * (n + 1)))
                pool.sem_inc(s["passed"], 1)
                pool.tensor_scalar(ve, var, EPS, None, ALU.add).then_inc(s[ve_sem], 1)
                pool.wait_ge(s[ve_sem], after(n + 1))
                pool.tensor_tensor(rs, ve, half_pow[:, :], ALU.pow).then_inc(s[rs_sem], 1)

            def a_stat(b, c, used):
                u = 2 * b + c
                pool.wait_ge(s["xh_done"], after(HT * (u - 1)))
                rstd_of(u, mv[:, c, :, 1], veps[:, :], rstd[:, c, :], "a_mv", "a_veps", "a_rstd")

            def a_split(b, c, used):
                u = 2 * b + c
                pool.wait_ge(s["qa_done"], after(u + 1))
                pool.wait_ge(s["q_mid"], after(u))
                pool.wait_ge(s["qb_done"], after(u + 1))
                pool.tensor_tensor(qr[:, :], qa[:, :], qb[:, :], ALU.add).then_inc(s["q_sum"], 1)
                pool.wait_ge(s["q_hi"], after(u + 1))
                pool.tensor_tensor(qr[:, :], qr[:, :], qp[:, c, 0, :], ALU.subtract).then_inc(s["q_rest"], 1)
                pool.wait_ge(s["q_mid"], after(u + 1))
                pool.tensor_tensor(qp[:, c, 2, :], qr[:, :], qp[:, c, 1, :], ALU.subtract).then_inc(s["q_lo"], 1)
                pool.wait_ge(s["q_lo"], after(u + 1))

            def turn_max(b, i, used):
                n = 4 * (NT * b + i)
                src, rest, part = nm[:, i % 2, :], nmr[:, i % 2, :], nmp[:, i % 2, :, :]
                pool.wait_ge(s[f"nm_rows{i % 2}"], after(48 * (NT // 2 * b + i // 2)))
                pool.wait_ge(s["nm_copied"], after(NT * b + i + 1))
                pool.sem_inc(s["passed"], 1)
                pool.tensor_copy(part[:, 0, :], src).then_inc(s["nm_steps"], 1)
                pool.wait_ge(s["nm_steps"], after(n + 1))
                pool.tensor_tensor(rest, src, part[:, 0, :], ALU.subtract).then_inc(s["nm_steps"], 1)
                pool.wait_ge(s["nm_steps"], after(n + 2))
                pool.sem_inc(s["passed"], 1)
                pool.tensor_copy(part[:, 1, :], rest).then_inc(s["nm_steps"], 1)
                pool.wait_ge(s["nm_steps"], after(n + 3))
                pool.tensor_tensor(part[:, 2, :], rest, part[:, 1, :], ALU.subtract).then_inc(s["nm_steps"], 1)
                pool.wait_ge(s["nm_steps"], after(n + 4))

            def o_rstd(k):
                def item(b, c, used):
                    rstd_of(3 * (2 * b + c) + k, omv[:, :, 1], oveps[:, :], orstd[:, :], "o_mv", "o_veps", "o_rstd")
                return item

            def o_n2(b, c, used):
                u = 2 * b + c
                pool.wait_ge(s["yn_done"], after(HT * (2 * u + 1)))
                pool.wait_ge(s["out_done"], after(u - 1))
                pool.wait_ge(s[f"xr_loaded{c}"], after(16 * (b + 1)))
                pool.tensor_tensor(x1[:, c, :, :], xr[:, c, :, :], y[:, c, :, :], ALU.add).then_inc(s["x1_done"], 1)

            def o_cT(b, c, used):
                pool.wait_ge(s["crow_done"], after(G * 16 * (2 * b + c + 1)))
                for e in range(SLOTS):
                    broadcast(b, c, e)

            def broadcast(b, c, e):
                k = G * (2 * b + c) + e
                pool.wait_ge(s["hs_done"], after(k - SLOTS + 1))
                pool.sem_inc(s["passed"], 1)
                pool.partition_broadcast(cb[:, e % SLOTS, :], crow[32 * (e % 4):32 * (e % 4) + 1, c, e // 4, :],
                                         P).then_inc(s["cb_done"], 1)
                pool.wait_ge(s["cb_done"], after(k + 1))

            def weigh(b, c, e):
                k = G * (2 * b + c) + e
                pool.wait_ge(s["ye_ps"], after(k - SLOTS + 1))
                pool.wait_ge(s["hg_done"], after(k + 1))
                pool.tensor_tensor(hs[:, e % SLOTS, :], hg[:, e % SLOTS, :], cb[:, e % SLOTS, :],
                                   ALU.mult).then_inc(s["hs_done"], 1)
                if e + SLOTS < G:
                    broadcast(b, c, e + SLOTS)

            def o_h(b, ce, used):
                c, e = ce
                if e < E:
                    weigh(b, c, e)

            def o_up(b, c, used):
                weigh(b, c, E)

            def o_n4(b, c, used):
                u = 2 * b + c
                pool.wait_ge(s["yn_done"], after(HT * (2 * u + 2)))
                pool.tensor_tensor(y[:, c, :, :], y[:, c, :, :], x1[:, c, :, :], ALU.add).then_inc(s["out_done"], 1)

            follow(pool, {"a_stat": a_stat, "a_split": a_split, "T": turn_max, "o_st2": o_rstd(0), "o_n2": o_n2,
                          "o_st3": o_rstd(1), "o_cT": o_cT, "o_h": o_h, "o_up": o_up, "o_st4": o_rstd(2), "o_n4": o_n4})

        @block.scalar
        def _(act):
            copy = nc.scalar.activation

            def a_turn(b, c, used):
                u = 2 * b + c
                act.wait_ge(s["x_written"], after(used + 1))
                copy(xT[:, c, :], psX[:, :], ACT.Copy).then_inc(s["x_read"], 1)

            def a_split(b, c, used):
                u = 2 * b + c
                act.wait_ge(s["q_sent"], after(16 * (u - 1)))
                act.wait_ge(s["q_sum"], after(u + 1))
                copy(qp[:, c, 0, :], qr[:, :], ACT.Copy).then_inc(s["q_hi"], 1)
                act.wait_ge(s["q_rest"], after(u + 1))
                copy(qp[:, c, 1, :], qr[:, :], ACT.Copy).then_inc(s["q_mid"], 1)

            def a_kT(b, c, used):
                act.wait_ge(s["KT_done"], after(NV * b))
                act.wait_ge(s["x_written"], after(used + 1))
                copy(KN[0:ROW_MAX, HALF * c:HALF * (c + 1)], psXb[0:ROW_MAX, 0:HALF], ACT.Copy).then_inc(s["x_read"], 1)
                act.wait_ge(s["x_read"], after(used + 1))
                act.sem_inc(s["KN_done"], 1)

            def scores(b, nr, used):
                n, r = nr
                if r == 0:
                    act.wait_ge(s["pv_done"], after(NSTEP * b + max(n - SLOTS + 1, 0)))
                act.wait_ge(s["s_ps"], after(NQ * b + NR * n + r + 1))
                nc.scalar.activation(pT[:, n % SLOTS, r, :], psS[:, r % 2, :], ACT.Exp,
                                     scale=float(D) ** -0.5).then_inc(s["exp_done"], 1)

            def evac(b, i, used):
                act.wait_ge(s[f"o_written{i % 2}"], after(N_OW * b + 128 * (i // 2)))
                act.wait_ge(s["pv_done"], after(NSTEP * b + STEPS.index((i, i)) + 1))
                copy(osb[:, i % 2, :], psO[:, :], ACT.Copy).then_inc(s["o_evac"], 1)

            def o_turn(b, c, used):
                act.wait_ge(s["x_written"], after(used + 1))
                copy(x2T[:, c, :], psX[:, :], ACT.Copy).then_inc(s["x_read"], 1)

            def o_rt(b, c, used):
                u = 2 * b + c
                act.wait_ge(s["ls_done"], after(u + 1))
                copy(ex[:, :, :], ls[:, :, :], ACT.Exp).then_inc(s["ex_done"], 1)
                copy(eg[:, :], lg[:, :, E], ACT.Exp, scale=-1.0).then_inc(s["ex_done"], 1)

            def o_cT(b, c, used):
                act.wait_ge(s["crow_done"], after(G * 16 * (2 * b + c)))
                act.wait_ge(s["x_written"], after(used + 1))
                copy(cT[:, :], psX[0:G * HT, 0:P], ACT.Copy).then_inc(s["x_read"], 1)
                act.wait_ge(s["x_read"], after(used + 1))
                act.sem_inc(s["cT_done"], 1)

            def o_h(b, ce, used):
                c, e = ce
                u = 2 * b + c
                act.wait_ge(s["sg_done"], after(G * u + e - SLOTS + 1))
                act.wait_ge(s["h_written"], after((G + 1) * u + e + 1))
                copy(th[:, e % SLOTS, :], psH[:, :], ACT.Tanh, scale=0.5).then_inc(s["th_done"], 1)

            follow(act, {"a_turn": a_turn, "a_split": a_split, "a_kT": a_kT, "S": scores, "evac": evac,
                         "o_turn": o_turn, "o_rt": o_rt, "o_cT": o_cT, "o_h": o_h})

        @block.tensor
        def _(pe):
            mm = nc.tensor.matmul

            def a_turn(b, c, used):
                pe.wait_ge(s["x_read"], after(used))
                for i in range(HT):
                    pe.wait_ge(s["xh_done"], after(HT * (2 * b + c) + i + 1))
                    t = pe.transpose(psX[:, P * i:P * (i + 1)], xh[:, c, i, :], ident[:, :])
                t.then_inc(s["x_written"], 1)

            def a_q(w):
                def item(b, c, used):
                    pe.wait_ge(s["x_read"], after(used))
                    mm(psX[:, :], wi[:, C * w:C * (w + 1)], xT[:, c, :], start=True, stop=True).then_inc(s["x_written"], 1)
                return item

            def a_kv(b, c, used):
                pe.wait_ge(s["x_read"], after(used))
                for i in range(HT):
                    kv = mm(psX[:, 3 * D * i:3 * D * (i + 1)], xT[:, c, P * i:P * (i + 1)],
                            wi[:, 2 * C:2 * C + 3 * D], start=True, stop=True)
                kv.then_inc(s["x_written"], 1)

            def a_kT(b, c, used):
                pe.wait_ge(s["x_read"], after(used))
                pe.wait_ge(s["kp_done"], after(3 * (2 * b + c + 1)))
                for i in range(HT):
                    t = pe.transpose(psXb[0:ROW_MAX, P * i:P * (i + 1)],
                                     kp[:, i, :, :, :].rearrange("p a k d -> p (a k d)"), identb[:, :])
                t.then_inc(s["x_written"], 1)

            def max_piece(b, n, used):
                i, heads, lo, hi = PIECES[n]
                if n == 0:
                    pe.wait_ge(s["q_rows0"], after(160 * (b + 1)))
                    pe.wait_ge(s["KN_done"], after(2 * b + 1))
                if n == OF_TILE[EARLY][0]:
                    pe.wait_ge(s["q_rows1"], after(160 * (b + 1)))
                    pe.wait_ge(s["KT_done"], after(NV * b + 1))
                pe.wait_ge(s["m_max"], after(NPIECE * b + max(n - 1, 0)))
                keys = KN[:, :] if i < EARLY else KT[:, 0, :]
                ps = psM[:, n % 2, 0:len(heads) * (hi - lo)].rearrange("p (h k) -> p h k", h=len(heads))
                diagonal = hi > P * i
                if diagonal:
                    mm(ps[:, :, hi - lo - P:hi - lo], identb[:, :],
                       tri[:, :].unsqueeze(1).to_broadcast([P, len(heads), P]), start=True, stop=False,
                       skip_group_check=True)
                for j, h in enumerate(heads):
                    m = mm(ps[:, j, :], QT[:, h, P * i:P * (i + 1)], keys[:, lo:hi], start=not diagonal,
                           stop=True, skip_group_check=diagonal)
                m.then_inc(s["m_ps"], 1)

            def turn_max(b, i, used):
                pe.wait_ge(s["x_read"], after(used))
                pe.wait_ge(s["m_block"], after(NT * b + i + 1))
                pe.transpose(psX[0:H, 0:P], nmx[:, i, :], ident[:, :]).then_inc(s["x_written"], 1)

            def scores(b, nr, used):
                n, r = nr
                i, kt = STEPS[n]
                if n == 0 and r == 0:
                    pe.wait_ge(s["KT_done"], after(NV * (b + 1)))
                if kt == 0 and r == 0:
                    pe.wait_ge(s[f"nm_rows{i % 2}"], after(48 * (NT // 2 * b + i // 2 + 1)))
                pe.wait_ge(s["exp_done"], after(NQ * b + max(NR * n + r - 1, 0)))
                t0 = P * i + QC * r
                v = 1 + r if kt == i else 0
                mm(psS[:, r % 2, :].rearrange("p (h t) -> p h t", h=H), KT[:, v, P * kt:P * (kt + 1)],
                   QT[:, :, t0:t0 + QC], start=True, stop=True).then_inc(s["s_ps"], 1)

            def values(b, n, used):
                i, kt = STEPS[n]
                if n == 0:
                    pe.wait_ge(s["vx_done"], after(b + 1))
                if kt == 0:
                    pe.wait_ge(s["o_evac"], after(NT * b + i))
                pe.wait_ge(s["exp_done"], after(NQ * b + NR * (n + 1)))
                for r in range(NR):
                    m = mm(psO[32 * r:32 * (r + 1), :], vx[:, kt, :], pT[:, n % SLOTS, r, :],
                           start=(kt == 0), stop=(kt == i))
                m.then_inc(s["pv_done"], 1)

            def o_proj(b, c, used):
                pe.wait_ge(s["x_read"], after(used))
                pe.wait_ge(s["aT_done"], after(2 * b + c + 1))
                for j in range(HT):
                    m = mm(psX[:, P * j:P * (j + 1)], aT[:, P * j:P * (j + 1)], wo[:, :], start=True, stop=True)
                m.then_inc(s["x_written"], 1)

            def o_turn(b, c, used):
                pe.wait_ge(s["x_read"], after(used))
                pe.wait_ge(s["xh2_done"], after(HT * (2 * b + c + 1)))
                for i in range(HT):
                    t = pe.transpose(psX[:, P * i:P * (i + 1)], xh2[:, i, :], ident[:, :])
                t.then_inc(s["x_written"], 1)

            def o_rt(b, c, used):
                pe.wait_ge(s["x_read"], after(used))
                for i in range(HT):
                    m = mm(psX[:, G * i:G * (i + 1)], x2T[:, c, P * i:P * (i + 1)], wr[:, :], start=True, stop=True)
                m.then_inc(s["x_written"], 1)

            def o_cT(b, c, used):
                pe.wait_ge(s["x_read"], after(used))
                pe.wait_ge(s["cmb_done"], after(2 * (2 * b + c + 1)))
                pe.sem_inc(s["passed"], 1)
                pe.transpose(psX[0:G * HT, 0:P], cmb[:, :, :].rearrange("p e i -> p (e i)"), ident[:, :]
                             ).then_inc(s["x_written"], 1)

            def hidden(u, j, c, w):
                pe.wait_ge(s["h_read"], after((G + 1) * u + j))
                mm(psH[:, :], w, x2T[:, c, :], start=True, stop=True).then_inc(s["h_written"], 1)

            def o_h(b, ce, used):
                c, e = ce
                hidden(2 * b + c, e, c, w1[:, e, :] if e < E else wgu[:, 0:C])

            def o_up(b, c, used):
                hidden(2 * b + c, G, c, wgu[:, C:2 * C])

            def o_y(b, ce, used):
                c, e = ce
                u = 2 * b + c
                if e == 0:
                    pe.wait_ge(s["yn_done"], after(HT * 2 * u))
                pe.wait_ge(s["hs_done"], after(G * u + e + 1))
                for j in range(HT):
                    m = mm(psY[:, P * j:P * (j + 1)], hs[:, e % SLOTS, P * j:P * (j + 1)],
                           w2[:, e, :] if e < E else wsd[:, :],
                           start=(e == 0 and j == 0), stop=(e == E), skip_group_check=True)
                m.then_inc(s["ye_ps"], 1)

            pe.wait_ge(s["const_p"], after(8))
            pe.wait_ge(s["w_loaded"], after(NW))

            first_piece = [True]

            def max_piece_first(b, n, used):
                if first_piece[0]:
                    pe.wait_ge(s["const_p"], after(NCP))
                    first_piece[0] = False
                max_piece(b, n, used)

            follow(pe, {"a_turn": a_turn, "a_q": a_q(0), "a_qs": a_q(1), "a_kv": a_kv, "a_kT": a_kT,
                        "M": max_piece_first, "T": turn_max, "S": scores, "V": values, "o_proj": o_proj,
                        "o_turn": o_turn, "o_rt": o_rt, "o_cT": o_cT, "o_h": o_h, "o_up": o_up, "o_y": o_y})

        @block.vector
        def _(dve):
            v = nc.vector
            v.memset(QT[:, :, :].bitcast(F32), 0.0).then_inc(s["const_v"], 1)
            v.memset(KT[:, :, :].bitcast(F32), 0.0).then_inc(s["const_v"], 1)
            v.memset(KN[:, :], 0.0).then_inc(s["const_v"], 1)
            v.memset(zrow[:, :], 0.0).then_inc(s["const_v"], 1)
            v.memset(vx[:, :, :], 0.0).then_inc(s["const_v"], 1)
            dve.wait_ge(s["const_v"], after(5))
            v.memset(KT[64:ROW_MASK, :, :], 1.0).then_inc(s["const_v"], 1)
            v.memset(KN[64:ROW_MASK, :], 1.0).then_inc(s["const_v"], 1)
            v.memset(vx[:, :, D:2 * D], 1.0).then_inc(s["vx_ones"], 1)

            def layer_stats(n, src, st, m_v, st_sem, mv_sem):
                for i in range(HT):
                    v.bn_stats(st[:, i, :], src(i)).then_inc(s[st_sem], 1)
                dve.wait_ge(s[st_sem], after(HT * (n + 1)))
                dve.sem_inc(s["passed"], 1)
                for i in range(HT):
                    v.bn_aggr(m_v[:, i, :], st[:, i, :]).then_inc(s[mv_sem], 1)

            def a_stat(b, c, used):
                u = 2 * b + c
                dve.wait_ge(s[f"x_loaded{c}"], after(16 * (b + 1)))
                layer_stats(u, lambda i: xt[:, c, i, :], stat, mv[:, c, :, :], "a_stat", "a_mv")

            def a_norm(b, c, used):
                u = 2 * b + c
                dve.wait_ge(s["a_rstd"], after(u + 1))
                for i in range(HT):
                    v.tensor_scalar(xh[:, c, i, :], xt[:, c, i, :], mv[:, c, i, 0:1], rstd[:, c, i:i + 1],
                                    ALU.subtract, ALU.mult).then_inc(s["xh_done"], 1)

            def a_q(w, dst, done):
                def item(b, c, used):
                    u = 2 * b + c
                    dve.wait_ge(s["q_sum"], after(u))
                    dve.wait_ge(s["x_written"], after(used + 1))
                    v.scalar_tensor_tensor(out=dst[:, :], in0=psX[:, :], scalar=bq[:, w:w + 1],
                                           in1=ropq[:, w, HALF * c:HALF * (c + 1)], op0=ALU.add, op1=ALU.mult
                                           ).then_inc(s["x_read"], 1)
                    dve.wait_ge(s["x_read"], after(used + 1))
                    dve.sem_inc(s[done], 1)
                return item

            def a_kv(b, c, used):
                kv = psX[:, 0:3 * D * HT].rearrange("p (i w d) -> p w i d", w=3, d=D)
                u = 2 * b + c
                n = 7 * u
                i0 = HT * c

                def bias(w):
                    return bkv[:, w, :].unsqueeze(1).to_broadcast([P, HT, D])

                dve.wait_ge(s["x_written"], after(used + 1))
                v.tensor_tensor(ka[:, :, :], kv[:, 0], bias(0), ALU.add).then_inc(s["k_steps"], 1)
                v.tensor_tensor(kb[:, :, :], kv[:, 1], bias(1), ALU.add).then_inc(s["k_steps"], 1)
                dve.wait_ge(s["vx_done"], after(b))
                v.tensor_tensor(vn[:, i0:i0 + HT, :], kv[:, 2], bias(2), ALU.add).then_inc(s["vn_done"], 1)
                dve.wait_ge(s["vn_done"], after(u + 1))
                dve.sem_inc(s["x_read"], 1)
                dve.wait_ge(s["k_steps"], after(n + 2))
                v.tensor_tensor(ka[:, :, :], ka[:, :, :], ropk[:, 0, i0:i0 + HT, :], ALU.mult).then_inc(s["k_steps"], 1)
                v.tensor_tensor(kb[:, :, :], kb[:, :, :], ropk[:, 1, i0:i0 + HT, :], ALU.mult).then_inc(s["k_steps"], 1)
                dve.wait_ge(s["k_steps"], after(n + 4))
                v.tensor_tensor(kr[:, :, :], ka[:, :, :], kb[:, :, :], ALU.add).then_inc(s["k_steps"], 1)

                def part(k):
                    return kp[:, :, :, k, :]

                def thrice(t):
                    return t[:, :, :].unsqueeze(2).to_broadcast([P, HT, PARTS, D])

                dve.wait_ge(s["k_steps"], after(n + 5))
                v.tensor_copy(part(0), thrice(kr)).then_inc(s["kp_done"], 1)
                dve.wait_ge(s["kp_done"], after(3 * u + 1))
                v.tensor_tensor(ka[:, :, :], kr[:, :, :], kp[:, :, 0, 0, :], ALU.subtract).then_inc(s["k_steps"], 1)
                dve.wait_ge(s["k_steps"], after(n + 6))
                v.tensor_copy(part(1), thrice(ka)).then_inc(s["kp_done"], 1)
                dve.wait_ge(s["kp_done"], after(3 * u + 2))
                v.tensor_tensor(part(2), thrice(ka), part(1), ALU.subtract).then_inc(s["kp_done"], 1)
                dve.sem_inc(s["k_steps"], 1)

            def keys(b, _, used):
                if isinstance(b, int) and b == 0:
                    dve.wait_ge(s["vx_ones"], after(1))
                dve.wait_ge(s["pv_done"], after(NSTEP * b))
                dve.wait_ge(s["vn_done"], after(2 * (b + 1)))
                v.tensor_copy(vx[:, :, 0:D], vn[:, :, :]).then_inc(s["vx_done"], 1)
                dve.wait_ge(s["KN_done"], after(2 * (b + 1)))
                for w in range(NV):
                    v.tensor_copy(KT[0:ROW_MAX, w, :], KN[0:ROW_MAX, :]).then_inc(s["KT_done"], 1)

            def max_piece(b, n, used):
                i, heads, lo, hi = PIECES[n]
                dve.wait_ge(s["m_ps"], after(NPIECE * b + n + 1))
                cut = nmx[:, i, :] if i < BT else nmx2[:, i - BT, lo // BANK, :]
                v.tensor_reduce(cut[:, heads[0]:heads[-1] + 1],
                                psM[:, n % 2, 0:len(heads) * (hi - lo)].rearrange("p (h k) -> p h k", h=len(heads)),
                                AX.X, ALU.max, negate=True).then_inc(s["m_max"], 1)
                if n == OF_TILE[i][-1]:
                    dve.wait_ge(s["m_max"], after(NPIECE * b + n + 1))
                    if i < BT:
                        dve.sem_inc(s["m_block"], 1)
                    else:
                        v.tensor_tensor(nmx[:, i, :], nmx2[:, i - BT, 0, :], nmx2[:, i - BT, 1, :],
                                        ALU.min).then_inc(s["m_block"], 1)

            def turn_max(b, i, used):
                dve.wait_ge(s["nm_steps"], after(4 * (NT * b + i - 1)))
                dve.wait_ge(s["x_written"], after(used + 1))
                v.tensor_copy(nm[:, i % 2, :], psX[0:H, 0:P]).then_inc(s["x_read"], 1)
                dve.wait_ge(s["x_read"], after(used + 1))
                dve.sem_inc(s["nm_copied"], 1)

            def o_div(b, c, used):
                u = 2 * b + c
                dve.wait_ge(s["inv_written"], after(16 * u))
                dve.wait_ge(s["den_read"], after(16 * (u + 1)))
                v.reciprocal(di[:, :], dn[:, :]).then_inc(s["den_inv"], 1)

            def o_aT(b, c, used):
                u = 2 * b + c
                dve.wait_ge(s["x_read"], after(used))
                dve.wait_ge(s["num_read"], after(16 * (u + 1)))
                dve.wait_ge(s["inv_read"], after(16 * (u + 1)))
                v.tensor_tensor(aT[:, :], oT[:, c, :], dT[:, :], ALU.mult).then_inc(s["aT_done"], 1)

            def o_proj(b, c, used):
                dve.wait_ge(s[f"stored{c}"], after(16 * b))
                dve.wait_ge(s["x_written"], after(used + 1))
                v.tensor_tensor(y[:, c, :, :], psX[:, :].rearrange("p (i n) -> p i n", n=C),
                                bo[:, :].unsqueeze(1).to_broadcast([P, HT, C]), ALU.add).then_inc(s["x_read"], 1)
                dve.wait_ge(s["x_read"], after(used + 1))

            def o_st2(b, c, used):
                u = 2 * b + c
                layer_stats(3 * u, lambda i: y[:, c, i, :], ostat, omv, "o_stat", "o_mv")

            def o_n2(b, c, used):
                u = 2 * b + c
                dve.wait_ge(s["o_rstd"], after(3 * u + 1))
                for i in range(HT):
                    v.tensor_scalar(y[:, c, i, :], y[:, c, i, :], omv[:, i, 0:1], orstd[:, i:i + 1],
                                    ALU.subtract, ALU.mult).then_inc(s["yn_done"], 1)

            def o_st3(b, c, used):
                u = 2 * b + c
                dve.wait_ge(s["x1_done"], after(u + 1))
                layer_stats(3 * u + 1, lambda i: x1[:, c, i, :], ostat, omv, "o_stat", "o_mv")

            def o_n3(b, c, used):
                u = 2 * b + c
                dve.wait_ge(s["o_rstd"], after(3 * u + 2))
                for i in range(HT):
                    v.tensor_scalar(xh2[:, i, :], x1[:, c, i, :], omv[:, i, 0:1], orstd[:, i:i + 1],
                                    ALU.subtract, ALU.mult).then_inc(s["xh2_done"], 1)

            def o_rt(b, c, used):
                u = 2 * b + c
                dve.wait_ge(s["x_written"], after(used + 1))
                v.tensor_copy(lg[:, :, :], psX[:, 0:G * HT].rearrange("p (i e) -> p i e", e=G)).then_inc(s["x_read"], 1)
                dve.wait_ge(s["x_read"], after(used + 1))
                v.tensor_reduce(red[:, :, 0], lg[:, :, 0:E], AX.X, ALU.max).then_inc(s["rt_steps"], 1)
                dve.wait_ge(s["rt_steps"], after(17 * u + 1))
                v.tensor_tensor(ls[:, :, :], lg[:, :, 0:E], red[:, :, :].to_broadcast([P, HT, E]),
                                ALU.subtract).then_inc(s["ls_done"], 1)

            def o_top(b, c, used):
                u = 2 * b + c
                step = [1]

                def then(ins):
                    ins.then_inc(s["rt_steps"], 1)
                    step[0] += 1
                    dve.wait_ge(s["rt_steps"], after(17 * u + step[0]))

                def wide(t):
                    return t[:, :, :].to_broadcast([P, HT, E])

                dve.wait_ge(s["ex_done"], after(2 * u + 2))
                then(v.tensor_reduce(red[:, :, 0], ex[:, :, :], AX.X, ALU.add))
                then(v.reciprocal(red[:, :, :], red[:, :, :]))
                then(v.tensor_tensor(pr[:, :, :], ex[:, :, :], wide(red), ALU.mult))
                then(v.tensor_reduce(red[:, :, 0], pr[:, :, :], AX.X, ALU.max))
                then(v.tensor_tensor(eq[:, :, :], pr[:, :, :], wide(red), ALU.is_equal))
                then(v.tensor_tensor(cand[:, :, :], eq[:, :, :], rank[:, :, :], ALU.mult))
                then(v.tensor_reduce(red[:, :, 0], cand[:, :, :], AX.X, ALU.max))
                then(v.tensor_tensor(oh1[:, :, :], cand[:, :, :], wide(red), ALU.is_equal))
                then(v.scalar_tensor_tensor(out=p2[:, :, :], in0=oh1[:, :, :], scalar=-2.0, in1=pr[:, :, :],
                                            op0=ALU.mult, op1=ALU.add))
                then(v.tensor_reduce(red[:, :, 0], p2[:, :, :], AX.X, ALU.max))
                then(v.tensor_tensor(eq[:, :, :], p2[:, :, :], wide(red), ALU.is_equal))
                then(v.tensor_tensor(cand[:, :, :], eq[:, :, :], rank[:, :, :], ALU.mult))
                then(v.tensor_reduce(red[:, :, 0], cand[:, :, :], AX.X, ALU.max))
                then(v.tensor_tensor(oh2[:, :, :], cand[:, :, :], wide(red), ALU.is_equal))
                then(v.tensor_tensor(oh1[:, :, :], oh1[:, :, :], oh2[:, :, :], ALU.add))
                then(v.tensor_scalar(eg[:, :], eg[:, :], 1.0, 2.0, ALU.add, ALU.mult))
                assert step[0] == 17
                v.reciprocal(cmb[:, E, :], eg[:, :]).then_inc(s["cmb_done"], 1)
                v.scalar_tensor_tensor(out=cmb[:, 0:E, :].rearrange("p e i -> p i e"), in0=pr[:, :, :], scalar=0.5,
                                       in1=oh1[:, :, :], op0=ALU.mult, op1=ALU.mult).then_inc(s["cmb_done"], 1)

            def gated(u, e, dst, done):
                dve.wait_ge(s["hs_done"], after(G * u + e - SLOTS + 1))
                dve.wait_ge(s["th_done"], after(G * u + e + 1))
                v.scalar_tensor_tensor(out=dst, in0=th[:, e % SLOTS, :], scalar=1.0, in1=psH[:, :],
                                       op0=ALU.add, op1=ALU.mult).then_inc(s["h_read"], 1)
                dve.wait_ge(s["h_read"], after((G + 1) * u + e + 1))
                dve.sem_inc(s["sg_done"], 1)

            def o_h(b, ce, used):
                c, e = ce
                u = 2 * b + c
                if e < E:
                    gated(u, e, hg[:, e % SLOTS, :], True)
                    dve.sem_inc(s["hg_done"], 1)
                else:
                    gated(u, e, shd[:, :], False)

            def o_up(b, c, used):
                u = 2 * b + c
                dve.wait_ge(s["h_written"], after((G + 1) * (u + 1)))
                v.tensor_tensor(hg[:, E % SLOTS, :], shd[:, :], psH[:, :], ALU.mult).then_inc(s["h_read"], 1)
                dve.wait_ge(s["h_read"], after((G + 1) * (u + 1)))
                dve.sem_inc(s["hg_done"], 1)

            def o_st4(b, c, used):
                u = 2 * b + c
                dve.wait_ge(s["ye_ps"], after(G * (u + 1)))
                layer_stats(3 * u + 2, lambda i: psY[:, P * i:P * (i + 1)], ostat, omv, "o_stat", "o_mv")

            def o_n4(b, c, used):
                u = 2 * b + c
                dve.wait_ge(s["x1_done"], after(u + 1))
                dve.wait_ge(s["o_rstd"], after(3 * u + 3))
                for i in range(HT):
                    v.tensor_scalar(y[:, c, i, :], psY[:, P * i:P * (i + 1)], omv[:, i, 0:1], orstd[:, i:i + 1],
                                    ALU.subtract, ALU.mult).then_inc(s["yn_done"], 1)

            dve.wait_ge(s["w_loaded"], after(NW))
            follow(dve, {"a_stat": a_stat, "a_norm": a_norm, "a_q": a_q(0, qa, "qa_done"), "a_qs": a_q(1, qb, "qb_done"),
                         "a_kv": a_kv, "keys": keys, "M": max_piece, "T": turn_max, "o_div": o_div, "o_aT": o_aT,
                         "o_proj": o_proj, "o_st2": o_st2, "o_n2": o_n2, "o_st3": o_st3, "o_n3": o_n3, "o_rt": o_rt,
                         "o_top": o_top, "o_h": o_h, "o_up": o_up, "o_st4": o_st4, "o_n4": o_n4})


def rope_tables():
    pos = np.arange(T, dtype=np.float32)
    freqs = (np.float32(1.0) / np.float32(10000.0) ** (np.arange(0, D, 2, dtype=np.float32) / np.float32(D))).astype(np.float32)
    ang = (pos[:, None] * freqs[None, :]).astype(np.float32)
    sin, cos = np.sin(ang), np.cos(ang)
    c = np.concatenate([cos, -cos], 1)
    n = np.concatenate([sin, sin], 1)
    q = np.stack([np.tile(c.T, (H, 1)), np.tile(n.T, (H, 1))], 1)
    k = np.stack([c.reshape(NT, P, D).transpose(1, 0, 2), n.reshape(NT, P, D).transpose(1, 0, 2)], 1)
    return np.ascontiguousarray(q, np.float32), np.ascontiguousarray(k, np.float32)


def kernel(L0_attn_x, L0_attn_Wq, L0_attn_bq, L0_attn_Wk, L0_attn_bk, L0_attn_Wv, L0_attn_bv, L0_attn_Wo, L0_attn_bo,
           L0_ffn_router_w, L0_ffn_w1, L0_ffn_w2, L0_ffn_shared_gate_up, L0_ffn_shared_down, L0_ffn_shared_gate_w):
    import concourse.bacc as bacc
    from concourse.bass_utils import run_bass_kernel_spmd

    def swap(w):
        w = np.asarray(w)
        return w.reshape(*w.shape[:-1], -1, 2, D // 2)[..., ::-1, :].reshape(w.shape)

    rope_q, rope_k = rope_tables()
    bkv = np.concatenate([np.asarray(L0_attn_bk), swap(L0_attn_bk), np.asarray(L0_attn_bv)]).reshape(1, 3, D)
    arrays = {
        "x": L0_attn_x,
        "w_in": np.concatenate([L0_attn_Wq, swap(L0_attn_Wq), L0_attn_Wk, swap(L0_attn_Wk), L0_attn_Wv], 1),
        "w_out": L0_attn_Wo,
        "b_q": np.stack([np.asarray(L0_attn_bq), swap(L0_attn_bq)], 1),
        "b_kv": np.broadcast_to(bkv, (P, 3, D)),
        "b_o": np.broadcast_to(np.asarray(L0_attn_bo)[None], (P, C)),
        "rope_q": rope_q,
        "rope_k": rope_k,
        "w_router": np.concatenate([L0_ffn_router_w, L0_ffn_shared_gate_w], 1),
        "w_up": L0_ffn_w1,
        "w_down": L0_ffn_w2,
        "w_gu": L0_ffn_shared_gate_up,
        "w_sd": L0_ffn_shared_down,
    }
    arrays = {n: np.ascontiguousarray(a) for n, a in arrays.items()}
    nc = bacc.Bacc("TRN2", target_bir_lowering=False, num_devices=1)
    args = [nc.dram_tensor(n, a.shape, F32, kind="ExternalInput").ap() for n, a in arrays.items()]
    out = nc.dram_tensor("out", (B, T, C), F32, kind="ExternalOutput").ap()
    build(nc, *args, out)
    r = run_bass_kernel_spmd(nc, [arrays], core_ids=[0])
    return r.results[0]["out"]
```

```python
from contextlib import ExitStack

import numpy as np

import concourse.bass as bass
from concourse import mybir

F32 = mybir.dt.float32
BF16 = mybir.dt.bfloat16
ALU = mybir.AluOpType
ACT = mybir.ActivationFunctionType
AX = mybir.AxisListType

P = 128
B, T, C = 4, 1024, 128
H, D = 16, 8
E = 8
G = E + 1
NT = T // P
QC = 32
NR = P // QC
NV = 1 + NR
BANK = 512
BT = BANK // P
HALF = T // 2
HT = HALF // P
PARTS = 3
ROW_MAX = PARTS * PARTS * D
ROW_MASK = 96
MASKED = -1e30
EPS = 1e-5
VW = 32
ROW_PARTS = 4
SLOTS = 3
EARLY = 4


def maximum_pieces():
    pieces = []
    for i in range(NT):
        lo, hi = BANK * (i // BT), P * (i + 1)
        if lo:
            pieces += [(i, [h], 0, lo) for h in range(H)]
        n = BANK // (hi - lo)
        pieces += [(i, list(range(h, h + n)), lo, hi) for h in range(0, H, n)]
    return pieces


PIECES = maximum_pieces()
NPIECE = len(PIECES)
OF_TILE = [[n for n, p in enumerate(PIECES) if p[0] == i] for i in range(NT)]
STEPS = [(i, kt) for i in range(NT) for kt in range(i + 1)]
NSTEP = len(STEPS)
LAST_OF_HALF = STEPS.index((NT - 1, HT - 1))
NQ = NR * NSTEP

USES_X = ("T", "a_turn", "a_q", "a_qs", "a_kv", "a_kT", "o_proj", "o_turn", "o_rt", "o_cT")

A_PLACES = {"a_stat": -0.258, "a_norm": 0.593, "a_turn": 1.143, "a_turn_out": 1.174, "a_q": 1.504, "a_q_out": 1.548, "a_qs": 1.92,
            "a_qs_out": 2.003, "a_sum": 2.462, "a_kv": 2.616, "a_kv_out": 2.746, "a_hi": 2.751, "a_rest": 2.986, "a_mid": 3.53,
            "a_lo": 3.676, "a_kT": 3.817, "a_kT_out": 4.001, "a_send": 4.304}
DIV_PLACES = {"o_load": -1.388, "o_div": -0.091, "o_inv": -0.085, "o_dT": -0.022}
O_PLACES = {"o_aT": -0.515, "o_proj": 0.08, "o_proj_out": 0.429, "o_st2": 0.444, "o_n2": 1.27, "o_st3": 1.79, "o_n3": 2.553,
            "o_turn": 2.918, "o_turn_out": 2.99, "o_rt": 3.255, "o_rt_out": 3.4, "o_ex": 3.839, "o_top": 3.896, "o_cT": 4.84,
            "o_cT_out": 4.996, "o_cb": 6.573}
EXPERT_PLACES = {"o_h": 0.197, "o_th": 0.276, "o_g": 0.4, "o_w": 0.994, "o_y": 1.96, "o_y2": 1.996}
END_PLACES = {"o_st4": 2.04, "o_n4": 2.978, "o_store": 3.014}
PLACES = {"hidden": 5.8, "pace": 0.75, "a_0": 7.865, "a_1": 12.751, "rows_0": 15.096, "div_0": 14.586, "o_0": 20.788,
          "div_1": 2.812, "o_1": 4.5, "late": 2.751, "late_rate": 4.6, "early": 25.617, "early_rate": 3.794, "V": 1.1,
          "evac": 1.139, "S": 0.2, "T": 0.611, "T_out": 0.084,
          "next_keys": 33.073, "first_keys": 0.537, "first_a": -5.509, "first_m": -4.711, "first_rate": 3.899, "ahead": 1.303}
VECTOR_TIME = {"keys": 1.8, "a_stat": 1.3, "a_q_out": 0.6, "a_qs_out": 0.6, "a_kv_out": 2.6,
               "T_out": 0.2, "o_div": 0.5, "o_aT": 0.6, "o_proj_out": 0.6, "o_st2": 1.3, "o_st3": 1.3,
               "o_rt_out": 0.6, "o_top": 3.0, "o_g": 0.6, "o_gu": 0.6, "o_st4": 1.3}


def a_items(d, c, at):
    return [(at + x, (name, d, c)) for name, x in A_PLACES.items()]


def o_items(d, c, div, at, ahead=0.0):
    items = [(div + x, (name, d, c)) for name, x in DIV_PLACES.items()]
    items += [(at + x, (name, d, c)) for name, x in O_PLACES.items()]
    for e in range(G):
        h = at + PLACES["hidden"] + PLACES["pace"] * (e + (e == E))
        x = EXPERT_PLACES
        if e == E:
            items += [(h - PLACES["pace"] + x[n], (n, d, (c, e))) for n in ("o_h", "o_th", "o_g")]
            items += [(h + x["o_h"], ("o_up", d, c)), (h + x["o_g"], ("o_gu", d, c))]
        else:
            items += [(h + x[n] - (ahead if e < SLOTS else 0.0), (n, d, (c, e))) for n in ("o_h", "o_th", "o_g")]
        items += [(h + x[n], (n, d, (c, e))) for n in ("o_w", "o_y", "o_y2")]
    return items + [(h + x, (name, d, c)) for name, x in END_PLACES.items()]


def order_of(placed):
    return [it for _, it in sorted(placed, key=lambda p: p[0])]


def taken_x(placed):
    place = {it: x for x, it in placed}
    return sorted((x, place[it[0] + "_out", *it[1:]]) for x, it in placed if it[0] in USES_X)


def clear(items, placed):
    while any(a <= d and c <= b for a, b in taken_x(items) for c, d in taken_x(placed)):
        items = [(x + 0.05, it) for x, it in items]
    return items


def maximum(d, tiles, start, rate, others):
    placed = []
    taken = taken_x(others)
    others = sorted((x, VECTOR_TIME[it[0]]) for x, it in others if x >= start and it[0] in VECTOR_TIME)
    at, room = start, 0.0
    for i in tiles:
        for n in OF_TILE[i]:
            _, heads, lo, hi = PIECES[n]
            while others and others[0][0] <= at:
                room -= others.pop(0)[1]
            while room < 0:
                at, room = at + 0.05, room + 0.05 * rate
                while others and others[0][0] <= at:
                    room -= others.pop(0)[1]
            placed.append((at, ("M", d, n)))
            room -= 0.07 + 0.00104 * len(heads) * (hi - lo)
        turn = at + PLACES["T"]
        for x, out in taken:
            if turn <= out and x <= turn + PLACES["T_out"]:
                turn = out + 0.01
        placed += [(turn, ("T", d, i)), (turn + PLACES["T_out"], ("T_out", d, i))]
    return placed


def body_order(first, last):
    p = PLACES
    placed = [(-1.0, ("a_rows", 0, 1)), (-1.0 if not first else p["first_keys"], ("keys", 0, 1))]
    if first:
        placed += [(-1.0, ("keys", 0, 0))]
    if not last:
        placed += [(p["next_keys"], ("keys", 1, 0))]
    if first:
        placed += clear(a_items(0, 1, p["first_a"]), placed)
        placed += [(-0.8, ("ready", 0, 0))]
    for n, (i, kt) in enumerate(STEPS):
        placed += [(n + p["S"] * r, ("S", 0, (n, r))) for r in range(NR)]
        placed += [(n + p["V"], ("V", 0, n))]
        if kt == i:
            placed += [(n + p["evac"], ("evac", 0, i))]
            if i % HT == HT - 1:
                placed += [(n + p["evac"] + 0.05, ("o_read", 0, i // HT))]
    if not first:
        placed += o_items(-1, 1, p["div_1"], p["o_1"])
    placed += clear(o_items(0, 0, p["div_0"], p["o_0"]), placed)
    if not last:
        placed += [(-0.9, ("a_load", 1, 0)), (-0.9, ("a_load", 1, 1))]
        placed += [(p["rows_0"], ("a_rows", 1, 0))] + clear(a_items(1, 0, p["a_0"]), placed)
        placed += clear(a_items(1, 1, p["a_1"]), placed)
    if first:
        early = maximum(0, range(EARLY), p["first_m"], p["first_rate"], placed)
        for i in range(EARLY):
            assert [x for x, it in early if it == ("T_out", 0, i)][0] < i * (i + 1) / 2
        placed += early
        p = {**p, "late": max(p["late"], early[-1][0])}
    late = maximum(0, range(EARLY, NT), p["late"], p["late_rate"], placed)
    for i in range(EARLY, NT):
        assert [x for x, it in late if it == ("T_out", 0, i)][0] < i * (i + 1) / 2
    if not last:
        placed += maximum(1, range(EARLY), max(late[-1][0], p["early"]), p["early_rate"], placed)
    return order_of(placed + late)


PROLOGUE = ([("a_load", 0, 0), ("a_load", 0, 1), ("load_first", 0, 0)]
            + order_of(a_items(0, 0, 0.0) + [
                (A_PLACES["a_stat"] + 0.01, ("zeros", 0, 0)), (A_PLACES["a_norm"] + 0.01, ("zeros", 0, 1)),
                (A_PLACES["a_turn_out"] + 0.01, ("zeros", 0, 2)), (A_PLACES["a_q"] - 0.01, ("first_loaded", 0, 0)),
                (A_PLACES["a_lo"] + 0.01, ("fill", 0, 0))])
            + [("a_rows", 0, 0), ("load_rest", 0, 0)])
FIRST, BODY, LAST = body_order(True, False), body_order(False, False), body_order(False, True)
TAIL = order_of(o_items(0, 1, 0.0, 1.0, PLACES["ahead"]))
LAST_U = 2 * B - 1


def uses_x(order):
    return sum(it[0] in USES_X for it in order)


def build(nc, x, w_in, w_out, b_q, b_kv, b_o, rope_q, rope_k, w_router, w_up, w_down, w_gu, w_sd, out):
    with ExitStack() as ctx:
        def sb(name, shape, dt=F32):
            return ctx.enter_context(nc.sbuf_tensor(name, shape, dt))

        def pb(name, shape, dt=F32):
            return ctx.enter_context(nc.psum_tensor(name, shape, dt))

        q_scr = nc.dram_tensor("q_scr", (2, PARTS, P, HALF), BF16, kind="Internal").ap()
        o_scr = nc.dram_tensor("o_scr", (2, H, D + 1, HALF), F32, kind="Internal").ap()
        inv_scr = nc.dram_tensor("inv_scr", (2, H, HALF), F32, kind="Internal").ap()

        wi = sb("wi", [P, 2 * C + 3 * D])
        wo = sb("wo", [P, C])
        bq = sb("bq", [P, 2])
        bkv = sb("bkv", [P, 3, D])
        bo = sb("bo", [P, C])
        ropq = sb("ropq", [P, 2, T])
        ropk = sb("ropk", [P, 2, NT, D])
        wr = sb("wr", [P, G])
        w1 = sb("w1", [P, E, C])
        w2 = sb("w2", [P, E, C])
        wgu = sb("wgu", [P, 2 * C])
        wsd = sb("wsd", [P, C])
        tri = sb("tri", [P, P], BF16)
        ident = sb("ident", [P, P])
        identb = sb("identb", [P, P], BF16)
        half_pow = sb("half_pow", [P, HT])
        rank = sb("rank", [P, HT, E])

        xt = sb("xt", [P, 2, HT, C])
        xh = sb("xh", [P, 2, HT, C])
        xT = sb("xT", [P, 2, HALF])
        stat = sb("stat", [P, HT, 6])
        mv = sb("mv", [P, 2, HT, 2])
        veps = sb("veps", [P, 2, HT])
        rstd = sb("rstd", [P, 2, 2, HT])
        qa = sb("qa", [P, HALF])
        qb = sb("qb", [P, HALF])
        qr = sb("qr", [P, HALF])
        qp = sb("qp", [P, 2, PARTS, HALF], BF16)
        ka = sb("ka", [P, HT, D])
        kb = sb("kb", [P, HT, D])
        kr = sb("kr", [P, HT, D])
        kp = sb("kp", [P, HT, PARTS, PARTS, D], BF16)
        QT = sb("QT", [P, H, T], BF16)
        KT = sb("KT", [P, NV, T], BF16)
        KN = sb("KN", [P, T], BF16)
        vx = sb("vx", [P, NT, VW])
        vn = sb("vn", [P, NT, D])
        nmx = sb("nmx", [P, NT, H])
        nmx2 = sb("nmx2", [P, NT // 2, 2, H])
        nm = sb("nm", [H, 2, P])
        nmr = sb("nmr", [H, 2, P])
        nmp = sb("nmp", [H, 2, PARTS, P], BF16)
        pT = sb("pT", [P, SLOTS, NR, BANK])
        osb = sb("osb", [P, 2, BANK])
        oT = sb("oT", [P, 2, HALF])
        dn = sb("dn", [P, H * HALF // P])
        di = sb("di", [P, H * HALF // P])
        dT = sb("dT", [P, HALF])
        aT = sb("aT", [P, HALF])
        xr = sb("xr", [P, 2, HT, C])
        y = sb("y", [P, 2, HT, C])
        x1 = sb("x1", [P, 2, HT, C])
        xh2 = sb("xh2", [P, HT, C])
        x2T = sb("x2T", [P, 2, HALF])
        ostat = sb("ostat", [P, HT, 6])
        omv = sb("omv", [P, HT, 2])
        oveps = sb("oveps", [P, 2, HT])
        orstd = sb("orstd", [P, 2, HT])
        lg = sb("lg", [P, HT, G])
        ls = sb("ls", [P, HT, E])
        ex = sb("ex", [P, HT, E])
        eg = sb("eg", [P, HT])
        pr = sb("pr", [P, HT, E])
        p2 = sb("p2", [P, HT, E])
        eq = sb("eq", [P, HT, E])
        cand = sb("cand", [P, HT, E])
        oh1 = sb("oh1", [P, HT, E])
        oh2 = sb("oh2", [P, HT, E])
        red = sb("red", [P, HT, 1])
        cmb = sb("cmb", [P, G, HT])
        cT = sb("cT", [G * HT, P])
        crow = sb("crow", [P, 2, 3, HALF])
        cb = sb("cb", [P, SLOTS, BANK])
        th = sb("th", [P, SLOTS, BANK])
        hg = sb("hg", [P, SLOTS, BANK])
        hs = sb("hs", [P, SLOTS, BANK])
        shd = sb("shd", [P, BANK])

        psS = pb("psS", [P, 2, BANK])
        psM = pb("psM", [P, 2, BANK])
        psO = pb("psO", [P, BANK])
        psX = pb("psX", [P, BANK])
        psH = pb("psH", [P, BANK])
        psY = pb("psY", [P, BANK])
        psXb = psX[:, :].bitcast(BF16)

        s = {n: ctx.enter_context(nc.semaphore(n)) for n in (
            "first_loaded", "w_loaded", "const_v", "const_a", "const_p", "x_loaded0", "x_loaded1", "xr_loaded0", "xr_loaded1",
            "x_written", "x_read",
            "a_stat", "a_mv", "a_veps", "a_rstd", "xh_done", "q_sum", "q_hi", "q_rest", "q_mid", "q_lo",
            "qa_done", "qb_done", "q_sent", "q_rows0", "q_rows1", "k_steps", "vn_done", "kp_done", "KN_done", "KT_done", "vx_done",
            "m_ps", "m_max", "m_block", "nm_copied", "nm_steps", "nm_rows0", "nm_rows1",
            "s_ps", "exp_done", "pv_done", "o_evac", "o_written0", "o_written1", "num_read", "den_read",
            "den_inv", "inv_written", "inv_read", "aT_done",
            "o_stat", "o_mv", "o_veps", "o_rstd", "yn_done", "x1_done", "xh2_done",
            "rt_steps", "ls_done", "ex_done", "cmb_done", "cT_done",
            "crow_done", "cb_done", "h_written", "h_read", "th_done", "sg_done", "hg_done", "hs_done", "ye_ps",
            "out_done", "stored0", "stored1", "passed")}

        names = list(s)
        with nc.Block() as start:
            for n, on in enumerate((start.sync, start.scalar, start.tensor, start.vector, start.gpsimd)):
                @on
                def _(eng, n=n):
                    for name in names[n::5]:
                        eng.sem_inc(s[name], 1)

        def after(count):
            return 1 + (max(count, 0) if isinstance(count, int) else count)


        def is_last(u):
            return isinstance(u, int) and u == LAST_U

        def hidden_bank(u, j):
            return (psS[:, j % 2, :], 2) if is_last(u) else (psH[:, :], 1)

        def follow(eng, items):
            def run(order, b, used):
                before = {}
                for name, d, what in order:
                    if name in USES_X:
                        before[name + "_out", d, what] = used
                    if name in items:
                        items[name](b + d, what, before.get((name, d, what), used))
                    if name in USES_X:
                        used = used + 1

            n0, n1, n2, n3 = (uses_x(o) for o in (PROLOGUE, FIRST, BODY, LAST))
            run(PROLOGUE, 0, 0)
            run(FIRST, 0, n0)
            with eng.Fori(1, B - 1) as b:
                run(BODY, b, n0 + n1 - n2 + n2 * b)
            run(LAST, B - 1, n0 + n1 + n2 * (B - 2))
            run(TAIL, B - 1, n0 + n1 + n2 * (B - 2) + n3)

        xb = x.rearrange("b (c i p) n -> b c p i n", p=P, c=2)
        ob = out.rearrange("b (c i p) n -> b c p i n", p=P, c=2)
        N_OW = NT // 2 * NR * 16
        FIRST_LOADS = [(wi[:, :], w_in), (bq[:, :], b_q), (ropq[:, :, :], rope_q), (bkv[:, :, :], b_kv),
                       (ropk[:, :, :, :], rope_k)]
        REST_LOADS = [(bo[:, :], b_o), (wo[:, :], w_out), (wr[:, :], w_router),
                      (w1[:, :, :], w_up.rearrange("e d f -> d e f")), (w2[:, :, :], w_down.rearrange("e f d -> f e d")),
                      (wgu[:, :], w_gu), (wsd[:, :], w_sd)]
        NQR = PARTS * PARTS * 16
        NCR = -(-G // ROW_PARTS) * 16
        NQF = 4
        NCV = 4
        NCP = 10 + NR

        block = ctx.enter_context(nc.Block())

        @block.sync
        def _(sp):
            def a_load(b, c, used):
                sp.wait_ge(s["xh_done"], after(HT * (2 * b + c - 1)))
                sp.sem_inc(s["passed"], 1)
                sp.dma_start(xt[:, c, :, :], xb[b, c]).then_inc(s[f"x_loaded{c}"], 16)

            def a_send(b, c, used):
                u = 2 * b + c
                sp.wait_ge(s["q_lo"], after(u + 1))
                sp.dma_start(q_scr[c].rearrange("a p t -> p a t"), qp[:, c, :, :]).then_inc(s["q_sent"], 16)

            def a_rows(b, c, used):
                u = 2 * b + c
                sp.wait_ge(s["s_ps"], after(NQ * (b - 1) + NR * (NSTEP if c else EARLY * (EARLY + 1) // 2)))
                sp.sem_inc(s["passed"], 1)
                t = slice(HALF * c, HALF * (c + 1))
                sp.wait_ge(s["q_sent"], after(16 * (u + 1)))
                for a in range(PARTS):
                    for k in range(PARTS):
                        r = (PARTS * a + k) * D
                        sp.dma_start(QT[r:r + D, :, t],
                                     q_scr[c, a].rearrange("(h j) t -> j h t", j=D)).then_inc(s[f"q_rows{c}"], 16)

            def turn_max(b, i, used):
                sp.wait_ge(s["nm_steps"], after(4 * (NT * b + i) + 4))
                for a in range(PARTS):
                    sp.dma_start(QT[ROW_MAX + a:ROW_MAX + a + 1, :, P * i:P * (i + 1)],
                                 nmp[:, i % 2, a, :]).then_inc(s[f"nm_rows{i % 2}"], 16)

            def evac(b, i, used):
                sp.wait_ge(s["o_evac"], after(NT * b + i + 1))
                c = i // HT
                for r in range(NR):
                    t = slice(P * (i % HT) + QC * r, P * (i % HT) + QC * (r + 1))
                    sp.dma_start(o_scr[c].rearrange("h d t -> d h t")[:, :, t],
                                 osb[32 * r:32 * r + D + 1, i % 2, :].rearrange("d (h t) -> d h t", h=H)
                                 ).then_inc(s[f"o_written{i % 2}"], 16)

            def o_read(b, c, used):
                u = 2 * b + c
                for w in range(2):
                    sp.wait_ge(s[f"o_written{w}"], after(N_OW * b + (N_OW // 2) * (c + 1)))
                    sp.sem_inc(s["passed"], 1)
                sp.wait_ge(s["den_inv"], after(u))
                sp.dma_start(dn[:, :], o_scr[c][:, D, :].rearrange("h (x t) -> h x t", x=P // H)).then_inc(s["den_read"], 16)
                sp.wait_ge(s["aT_done"], after(u - 1))
                sp.dma_start(oT[:, c, :], o_scr[c][:, 0:D, :]).then_inc(s["num_read"], 16)

            def o_inv(b, c, used):
                u = 2 * b + c
                sp.wait_ge(s["den_inv"], after(u + 1))
                sp.dma_start(inv_scr[c].rearrange("h (x t) -> (h x) t", x=P // H), di[:, :]).then_inc(s["inv_written"], 16)

            def o_dT(b, c, used):
                u = 2 * b + c
                sp.wait_ge(s["inv_written"], after(16 * (u + 1)))
                sp.sem_inc(s["passed"], 1)
                sp.wait_ge(s["aT_done"], after(u))
                sp.dma_start(dT[:, :], inv_scr[c].unsqueeze(1).to_broadcast([H, D, HALF])).then_inc(s["inv_read"], 16)

            def o_load(b, c, used):
                sp.wait_ge(s["x1_done"], after(2 * b + c - 1))
                sp.sem_inc(s["passed"], 1)
                sp.dma_start(xr[:, c, :, :], xb[b, c]).then_inc(s[f"xr_loaded{c}"], 16)

            def o_cT(b, c, used):
                u = 2 * b + c
                sp.wait_ge(s["cT_done"], after(u + 1))
                sp.sem_inc(s["passed"], 1)
                sp.wait_ge(s["cb_done"], after(G * (u - 1)))
                for e in range(0, G, ROW_PARTS):
                    n = min(ROW_PARTS, G - e)
                    sp.dma_start(crow[0:32 * (n - 1) + 1:32, c, e // ROW_PARTS, :].rearrange("e (i t) -> e i t", t=P),
                                 cT[HT * e:HT * (e + n), :]).then_inc(s["crow_done"], 16)

            def o_store(b, c, used):
                sp.wait_ge(s["out_done"], after(2 * b + c + 1))
                sp.sem_inc(s["passed"], 1)
                sp.dma_start(ob[b, c], y[:, c, :, :]).then_inc(s[f"stored{c}"], 16)

            def load_first(b, _, used):
                for dst, src in FIRST_LOADS:
                    sp.dma_start(dst, src).then_inc(s["first_loaded"], 16)

            def load_rest(b, _, used):
                for dst, src in REST_LOADS:
                    sp.dma_start(dst, src).then_inc(s["w_loaded"], 16)

            def a_rows_start(b, c, used):
                if isinstance(b, int) and b == 0:
                    sp.wait_ge(s["const_v"], after(c + 1))
                a_rows(b, c, used)

            follow(sp, {"a_load": a_load, "load_first": load_first, "load_rest": load_rest, "a_send": a_send,
                        "a_rows": a_rows_start, "T_out": turn_max, "evac": evac, "o_read": o_read,
                        "o_inv": o_inv, "o_dT": o_dT, "o_load": o_load, "o_cT_out": o_cT, "o_store": o_store})
            for c in range(2):
                sp.wait_ge(s[f"stored{c}"], after(16 * B))

        @block.gpsimd
        def _(pool):
            pool.memset(ident[:, :], 0.0).then_inc(s["const_p"], 1)
            pool.memset(identb[:, :], 0.0).then_inc(s["const_p"], 1)
            pool.memset(tri[:, :], 0.0).then_inc(s["const_p"], 1)
            pool.memset(half_pow[:, :], -0.5).then_inc(s["const_p"], 1)
            pool.wait_ge(s["const_p"], after(4))
            pool.affine_select(out=ident[:, :], in_=ident[:, :], compare_op=ALU.not_equal, fill=1.0,
                               base=0, pattern=[[-1, P]], channel_multiplier=1).then_inc(s["const_p"], 1)
            pool.affine_select(out=identb[:, :], in_=identb[:, :], compare_op=ALU.not_equal, fill=1.0,
                               base=0, pattern=[[-1, P]], channel_multiplier=1).then_inc(s["const_p"], 1)
            pool.affine_select(out=tri[:, :], in_=tri[:, :], compare_op=ALU.is_ge, fill=MASKED,
                               base=0, pattern=[[-1, P]], channel_multiplier=1).then_inc(s["const_p"], 1)
            pool.iota(rank[:, :, :], pattern=[[0, HT], [-1, E]], base=E, channel_multiplier=0,
                      allow_small_or_imprecise_dtypes=True).then_inc(s["const_p"], 1)
            pool.wait_ge(s["const_p"], after(8))

            def zeros(b, stage, used):
                if stage == 0:
                    pool.wait_ge(s["a_rstd"], after(1))
                    pool.memset(KT[64:ROW_MASK, :, :], 1.0).then_inc(s["const_p"], 1)
                    pool.wait_ge(s["const_p"], after(9))
                    pool.memset(KT[ROW_MASK:P, :, :], 0.0).then_inc(s["const_p"], 1)
                    pool.wait_ge(s["const_p"], after(10))

            def fill(b, _, used):
                pool.wait_ge(s["q_lo"], after(1))
                for v in range(1, NV):
                    m = KT[ROW_MASK:P, v, :].rearrange("p (i k) -> p i k", k=P)
                    pool.affine_select(out=m, in_=m, compare_op=ALU.is_ge, fill=MASKED, base=QC * (v - 1),
                                       pattern=[[0, NT], [-1, P]], channel_multiplier=1).then_inc(s["const_p"], 1)
                    pool.wait_ge(s["const_p"], after(10 + v))

            def scale_of(n, m_v, steps, rs, mv_sem, step_sem, rs_sem):
                ve, neg = steps[:, 0, :], steps[:, 1, :]
                pool.wait_ge(s[mv_sem], after(HT * (n + 1)))
                pool.sem_inc(s["passed"], 1)
                pool.tensor_scalar(ve, m_v[:, :, 1], EPS, None, ALU.add).then_inc(s[step_sem], 1)
                pool.tensor_scalar(neg, m_v[:, :, 0], -1.0, None, ALU.mult).then_inc(s[step_sem], 1)
                pool.wait_ge(s[step_sem], after(3 * n + 2))
                pool.tensor_tensor(rs[:, 0, :], ve, half_pow[:, :], ALU.pow).then_inc(s[step_sem], 1)
                pool.wait_ge(s[step_sem], after(3 * n + 3))
                pool.tensor_tensor(rs[:, 1, :], neg, rs[:, 0, :], ALU.mult).then_inc(s[rs_sem], 1)

            def a_stat(b, c, used):
                u = 2 * b + c
                pool.wait_ge(s["xh_done"], after(HT * (u - 1)))
                scale_of(u, mv[:, c, :, :], veps, rstd[:, c, :, :], "a_mv", "a_veps", "a_rstd")

            def a_sum(b, c, used):
                u = 2 * b + c
                pool.wait_ge(s["qa_done"], after(u + 1))
                pool.wait_ge(s["q_lo"], after(u))
                pool.wait_ge(s["qb_done"], after(u + 1))
                pool.tensor_tensor(qr[:, :], qa[:, :], qb[:, :], ALU.add).then_inc(s["q_sum"], 1)

            def a_rest(b, c, used):
                u = 2 * b + c
                pool.wait_ge(s["q_hi"], after(u + 1))
                pool.tensor_tensor(qr[:, :], qr[:, :], qp[:, c, 0, :], ALU.subtract).then_inc(s["q_rest"], 1)

            def a_lo(b, c, used):
                u = 2 * b + c
                pool.wait_ge(s["q_mid"], after(u + 1))
                pool.tensor_tensor(qp[:, c, 2, :], qr[:, :], qp[:, c, 1, :], ALU.subtract).then_inc(s["q_lo"], 1)

            def turn_max(b, i, used):
                n = 4 * (NT * b + i)
                src, rest, part = nm[:, i % 2, :], nmr[:, i % 2, :], nmp[:, i % 2, :, :]
                pool.wait_ge(s[f"nm_rows{i % 2}"], after(48 * (NT // 2 * b + i // 2)))
                pool.wait_ge(s["nm_copied"], after(NT * b + i + 1))
                pool.sem_inc(s["passed"], 1)
                pool.tensor_copy(part[:, 0, :], src).then_inc(s["nm_steps"], 1)
                pool.wait_ge(s["nm_steps"], after(n + 1))
                pool.tensor_tensor(rest, src, part[:, 0, :], ALU.subtract).then_inc(s["nm_steps"], 1)
                pool.wait_ge(s["nm_steps"], after(n + 2))
                pool.sem_inc(s["passed"], 1)
                pool.tensor_copy(part[:, 1, :], rest).then_inc(s["nm_steps"], 1)
                pool.wait_ge(s["nm_steps"], after(n + 3))
                pool.tensor_tensor(part[:, 2, :], rest, part[:, 1, :], ALU.subtract).then_inc(s["nm_steps"], 1)
                pool.wait_ge(s["nm_steps"], after(n + 4))

            def o_rstd(k):
                def item(b, c, used):
                    scale_of(3 * (2 * b + c) + k, omv, oveps, orstd, "o_mv", "o_veps", "o_rstd")
                return item

            def o_n2(b, c, used):
                u = 2 * b + c
                pool.wait_ge(s["yn_done"], after(HT * (2 * u + 1)))
                pool.wait_ge(s["out_done"], after(u - 1))
                pool.wait_ge(s[f"xr_loaded{c}"], after(16 * (b + 1)))
                pool.tensor_tensor(x1[:, c, :, :], xr[:, c, :, :], y[:, c, :, :], ALU.add).then_inc(s["x1_done"], 1)

            def o_cb(b, c, used):
                pool.wait_ge(s["crow_done"], after(NCR * (2 * b + c + 1)))
                for e in range(SLOTS):
                    broadcast(b, c, e)

            def broadcast(b, c, e):
                k = G * (2 * b + c) + e
                pool.wait_ge(s["hs_done"], after(k - SLOTS + 1))
                pool.sem_inc(s["passed"], 1)
                pool.partition_broadcast(cb[:, e % SLOTS, :], crow[32 * (e % ROW_PARTS):32 * (e % ROW_PARTS) + 1, c, e // ROW_PARTS, :],
                                         P).then_inc(s["cb_done"], 1)
                pool.wait_ge(s["cb_done"], after(k + 1))

            def o_w(b, ce, used):
                c, e = ce
                k = G * (2 * b + c) + e
                if not is_last(2 * b + c):
                    pool.wait_ge(s["ye_ps"], after(k - SLOTS + 1))
                    pool.wait_ge(s["hg_done"], after(k + 1))
                    pool.tensor_tensor(hs[:, e % SLOTS, :], hg[:, e % SLOTS, :], cb[:, e % SLOTS, :],
                                       ALU.mult).then_inc(s["hs_done"], 1)
                if e + SLOTS < G:
                    broadcast(b, c, e + SLOTS)

            def o_n4(b, c, used):
                u = 2 * b + c
                pool.wait_ge(s["yn_done"], after(HT * (2 * u + 2)))
                pool.tensor_tensor(y[:, c, :, :], y[:, c, :, :], x1[:, c, :, :], ALU.add).then_inc(s["out_done"], 1)

            follow(pool, {"zeros": zeros, "fill": fill, "a_stat": a_stat, "a_sum": a_sum, "a_rest": a_rest, "a_lo": a_lo, "T_out": turn_max,
                          "o_st2": o_rstd(0), "o_n2": o_n2, "o_st3": o_rstd(1), "o_cb": o_cb, "o_w": o_w,
                          "o_st4": o_rstd(2), "o_n4": o_n4})

        @block.scalar
        def _(act):
            copy = nc.scalar.activation

            def norm(dst, src, rs, i):
                return nc.scalar.activation(dst, src, ACT.Identity, bias=rs[:, 1, i:i + 1], scale=rs[:, 0, i:i + 1])

            def a_norm(b, c, used):
                act.wait_ge(s["a_rstd"], after(2 * b + c + 1))
                for i in range(HT):
                    norm(xh[:, c, i, :], xt[:, c, i, :], rstd[:, c, :, :], i).then_inc(s["xh_done"], 1)

            def o_n2(b, c, used):
                act.wait_ge(s["o_rstd"], after(3 * (2 * b + c) + 1))
                for i in range(HT):
                    norm(y[:, c, i, :], y[:, c, i, :], orstd, i).then_inc(s["yn_done"], 1)

            def o_n3(b, c, used):
                act.wait_ge(s["o_rstd"], after(3 * (2 * b + c) + 2))
                for i in range(HT):
                    norm(xh2[:, i, :], x1[:, c, i, :], orstd, i).then_inc(s["xh2_done"], 1)

            def o_n4(b, c, used):
                act.wait_ge(s["o_rstd"], after(3 * (2 * b + c) + 3))
                for i in range(HT):
                    norm(y[:, c, i, :], psY[:, P * i:P * (i + 1)], orstd, i).then_inc(s["yn_done"], 1)

            def a_turn(b, c, used):
                u = 2 * b + c
                act.wait_ge(s["x_written"], after(used + 1))
                copy(xT[:, c, :], psX[:, :], ACT.Copy).then_inc(s["x_read"], 1)

            def a_hi(b, c, used):
                u = 2 * b + c
                act.wait_ge(s["q_sent"], after(16 * (u - 1)))
                act.wait_ge(s["q_sum"], after(u + 1))
                copy(qp[:, c, 0, :], qr[:, :], ACT.Copy).then_inc(s["q_hi"], 1)

            def a_mid(b, c, used):
                act.wait_ge(s["q_rest"], after(2 * b + c + 1))
                copy(qp[:, c, 1, :], qr[:, :], ACT.Copy).then_inc(s["q_mid"], 1)

            def zeros(b, stage, used):
                if stage == 0:
                    act.wait_ge(s["const_p"], after(8))
                for k in range(stage, stage + 2) if stage != 1 else ():
                    h = slice(H // NQF * k, H // NQF * (k + 1))
                    copy(QT[ROW_MASK:P, h, :].rearrange("p h (c t) -> p (h c) t", t=QC),
                         identb[ROW_MASK:P, ROW_MASK:P].unsqueeze(1).to_broadcast([QC, H // NQF * T // QC, QC]),
                         ACT.Copy).then_inc(s["const_a"], 1)

            def a_kT(b, c, used):
                act.wait_ge(s["KT_done"], after(2 * NV * b))
                act.wait_ge(s["x_written"], after(used + 1))
                copy(KN[0:ROW_MAX, HALF * c:HALF * (c + 1)], psXb[0:ROW_MAX, 0:HALF], ACT.Copy).then_inc(s["x_read"], 1)
                act.wait_ge(s["x_read"], after(used + 1))
                act.sem_inc(s["KN_done"], 1)

            def scores(b, nr, used):
                n, r = nr
                if r == 0:
                    act.wait_ge(s["pv_done"], after(NSTEP * b + max(n - SLOTS + 1, 0)))
                act.wait_ge(s["s_ps"], after(NQ * b + NR * n + r + 1))
                nc.scalar.activation(pT[:, n % SLOTS, r, :], psS[:, r % 2, :], ACT.Exp,
                                     scale=float(D) ** -0.5).then_inc(s["exp_done"], 1)

            def evac(b, i, used):
                act.wait_ge(s[f"o_written{i % 2}"], after(N_OW * b + 16 * NR * (i // 2)))
                act.wait_ge(s["pv_done"], after(NSTEP * b + STEPS.index((i, i)) + 1))
                copy(osb[:, i % 2, :], psO[:, :], ACT.Copy).then_inc(s["o_evac"], 1)

            def o_turn(b, c, used):
                act.wait_ge(s["x_written"], after(used + 1))
                copy(x2T[:, c, :], psX[:, :], ACT.Copy).then_inc(s["x_read"], 1)

            def o_ex(b, c, used):
                u = 2 * b + c
                act.wait_ge(s["ls_done"], after(u + 1))
                copy(ex[:, :, :], ls[:, :, :], ACT.Exp).then_inc(s["ex_done"], 1)
                copy(eg[:, :], lg[:, :, E], ACT.Exp, scale=-1.0).then_inc(s["ex_done"], 1)

            def o_cT(b, c, used):
                act.wait_ge(s["crow_done"], after(NCR * (2 * b + c)))
                act.wait_ge(s["x_written"], after(used + 1))
                copy(cT[:, :], psX[0:G * HT, 0:P], ACT.Copy).then_inc(s["x_read"], 1)
                act.wait_ge(s["x_read"], after(used + 1))
                act.sem_inc(s["cT_done"], 1)

            def o_th(b, ce, used):
                c, e = ce
                u = 2 * b + c
                act.wait_ge(s["sg_done"], after(G * u + e - SLOTS + 1))
                act.wait_ge(s["h_written"], after((G + 1) * u + e + 1))
                copy(th[:, e % SLOTS, :], hidden_bank(u, e)[0], ACT.Tanh, scale=0.5).then_inc(s["th_done"], 1)

            follow(act, {"a_norm": a_norm, "o_n2": o_n2, "o_n3": o_n3, "o_n4": o_n4, "zeros": zeros, "a_turn_out": a_turn, "a_hi": a_hi, "a_mid": a_mid, "a_kT_out": a_kT,
                         "S": scores, "evac": evac, "o_turn_out": o_turn, "o_ex": o_ex, "o_cT_out": o_cT, "o_th": o_th})

        @block.tensor
        def _(pe):
            mm = nc.tensor.matmul

            def a_turn(b, c, used):
                pe.wait_ge(s["x_read"], after(used))
                for i in range(HT):
                    pe.wait_ge(s["xh_done"], after(HT * (2 * b + c) + i + 1))
                    t = pe.transpose(psX[:, P * i:P * (i + 1)], xh[:, c, i, :], ident[:, :])
                t.then_inc(s["x_written"], 1)

            def a_q(w):
                def item(b, c, used):
                    pe.wait_ge(s["x_read"], after(used))
                    mm(psX[:, :], wi[:, C * w:C * (w + 1)], xT[:, c, :], start=True, stop=True).then_inc(s["x_written"], 1)
                return item

            def a_kv(b, c, used):
                pe.wait_ge(s["x_read"], after(used))
                for i in range(HT):
                    kv = mm(psX[:, 3 * D * i:3 * D * (i + 1)], xT[:, c, P * i:P * (i + 1)],
                            wi[:, 2 * C:2 * C + 3 * D], start=True, stop=True)
                kv.then_inc(s["x_written"], 1)

            def a_kT(b, c, used):
                pe.wait_ge(s["x_read"], after(used))
                pe.wait_ge(s["kp_done"], after(3 * (2 * b + c + 1)))
                for i in range(HT):
                    t = pe.transpose(psXb[0:ROW_MAX, P * i:P * (i + 1)],
                                     kp[:, i, :, :, :].rearrange("p a k d -> p (a k d)"), identb[:, :])
                t.then_inc(s["x_written"], 1)

            def max_piece(b, n, used):
                i, heads, lo, hi = PIECES[n]
                if n == 0:
                    pe.wait_ge(s["q_rows0"], after(NQR * (b + 1)))
                    pe.wait_ge(s["KN_done"], after(2 * b + 1))
                if n == OF_TILE[EARLY][0]:
                    pe.wait_ge(s["q_rows1"], after(NQR * (b + 1)))
                    pe.wait_ge(s["KT_done"], after(NV * (2 * b + 1) + 1))
                pe.wait_ge(s["m_max"], after(NPIECE * b + max(n - 1, 0)))
                keys = KN[0:ROW_MAX, :] if i < EARLY else KT[0:ROW_MAX, 0, :]
                ps = psM[:, n % 2, 0:len(heads) * (hi - lo)].rearrange("p (h k) -> p h k", h=len(heads))
                diagonal = hi > P * i
                if diagonal:
                    mm(ps[:, :, hi - lo - P:hi - lo], identb[:, :],
                       tri[:, :].unsqueeze(1).to_broadcast([P, len(heads), P]), start=True, stop=False,
                       skip_group_check=True)
                for j, h in enumerate(heads):
                    m = mm(ps[:, j, :], QT[0:ROW_MAX, h, P * i:P * (i + 1)], keys[:, lo:hi], start=not diagonal,
                           stop=True, skip_group_check=diagonal)
                m.then_inc(s["m_ps"], 1)

            def turn_max(b, i, used):
                pe.wait_ge(s["x_read"], after(used))
                pe.wait_ge(s["m_block"], after(NT * b + i + 1))
                pe.transpose(psX[0:H, 0:P], nmx[:, i, :], ident[:, :]).then_inc(s["x_written"], 1)

            def scores(b, nr, used):
                n, r = nr
                i, kt = STEPS[n]
                if n == 0 and r == 0:
                    pe.wait_ge(s["KT_done"], after(NV * (2 * b + 1)))
                if n == STEPS.index((HT, 0)) and r == 0:
                    pe.wait_ge(s["q_rows1"], after(NQR * (b + 1)))
                    pe.wait_ge(s["KT_done"], after(NV * (2 * b + 2)))
                if kt == 0 and r == 0:
                    pe.wait_ge(s[f"nm_rows{i % 2}"], after(48 * (NT // 2 * b + i // 2 + 1)))
                pe.wait_ge(s["exp_done"], after(NQ * b + max(NR * n + r - 1, 0)))
                t0 = P * i + QC * r
                v = 1 + r if kt == i else 0
                mm(psS[:, r % 2, :].rearrange("p (h t) -> p h t", h=H), KT[:, v, P * kt:P * (kt + 1)],
                   QT[:, :, t0:t0 + QC], start=True, stop=True).then_inc(s["s_ps"], 1)

            def values(b, n, used):
                i, kt = STEPS[n]
                if n == 0:
                    pe.wait_ge(s["vx_done"], after(2 * b + 1))
                if n == STEPS.index((HT, 0)):
                    pe.wait_ge(s["vx_done"], after(2 * b + 2))
                if kt == 0:
                    pe.wait_ge(s["o_evac"], after(NT * b + i))
                pe.wait_ge(s["exp_done"], after(NQ * b + NR * (n + 1)))
                for r in range(NR):
                    m = mm(psO[32 * r:32 * (r + 1), :], vx[:, kt, :], pT[:, n % SLOTS, r, :],
                           start=(kt == 0), stop=(kt == i))
                m.then_inc(s["pv_done"], 1)

            def o_proj(b, c, used):
                pe.wait_ge(s["x_read"], after(used))
                pe.wait_ge(s["aT_done"], after(2 * b + c + 1))
                for j in range(HT):
                    m = mm(psX[:, P * j:P * (j + 1)], aT[:, P * j:P * (j + 1)], wo[:, :], start=True, stop=True)
                m.then_inc(s["x_written"], 1)

            def o_turn(b, c, used):
                pe.wait_ge(s["x_read"], after(used))
                pe.wait_ge(s["xh2_done"], after(HT * (2 * b + c + 1)))
                for i in range(HT):
                    t = pe.transpose(psX[:, P * i:P * (i + 1)], xh2[:, i, :], ident[:, :])
                t.then_inc(s["x_written"], 1)

            def o_rt(b, c, used):
                pe.wait_ge(s["x_read"], after(used))
                for i in range(HT):
                    m = mm(psX[:, G * i:G * (i + 1)], x2T[:, c, P * i:P * (i + 1)], wr[:, :], start=True, stop=True)
                m.then_inc(s["x_written"], 1)

            def o_cT(b, c, used):
                pe.wait_ge(s["x_read"], after(used))
                pe.wait_ge(s["cmb_done"], after(2 * (2 * b + c + 1)))
                pe.sem_inc(s["passed"], 1)
                pe.transpose(psX[0:G * HT, 0:P], cmb[:, :, :].rearrange("p e i -> p (e i)"), ident[:, :]
                             ).then_inc(s["x_written"], 1)

            def hidden(u, j, c, w):
                bank, n = hidden_bank(u, j)
                pe.wait_ge(s["h_read"], after((G + 1) * u + j + 1 - n))
                mm(bank, w, x2T[:, c, :], start=True, stop=True).then_inc(s["h_written"], 1)

            def o_h(b, ce, used):
                c, e = ce
                hidden(2 * b + c, e, c, w1[:, e, :] if e < E else wgu[:, 0:C])

            def o_up(b, c, used):
                hidden(2 * b + c, G, c, wgu[:, C:2 * C])

            def output(u, e, tiles):
                for j in tiles:
                    m = mm(psY[:, P * j:P * (j + 1)], hs[:, e % SLOTS, P * j:P * (j + 1)],
                           w2[:, e, :] if e < E else wsd[:, :],
                           start=(e == 0 and j == 0), stop=(e == E), skip_group_check=True)
                return m

            def o_y(b, ce, used):
                c, e = ce
                u = 2 * b + c
                if e == 0:
                    pe.wait_ge(s["yn_done"], after(HT * 2 * u))
                pe.wait_ge(s["hs_done"], after(G * u + e + 1))
                output(u, e, range(HT // 2))

            def o_y2(b, ce, used):
                c, e = ce
                output(2 * b + c, e, range(HT // 2, HT)).then_inc(s["ye_ps"], 1)

            def first_loaded(b, _, used):
                pe.wait_ge(s["first_loaded"], after(16 * len(FIRST_LOADS)))

            def ready(b, _, used):
                pe.wait_ge(s["const_p"], after(NCP))
                pe.wait_ge(s["const_a"], after(NQF))
                pe.wait_ge(s["const_v"], after(NCV))
                pe.wait_ge(s["w_loaded"], after(16 * len(REST_LOADS)))

            pe.wait_ge(s["const_p"], after(8))
            follow(pe, {"first_loaded": first_loaded, "ready": ready, "a_turn": a_turn, "a_q": a_q(0), "a_qs": a_q(1), "a_kv": a_kv, "a_kT": a_kT,
                        "M": max_piece, "T": turn_max, "S": scores, "V": values, "o_proj": o_proj,
                        "o_turn": o_turn, "o_rt": o_rt, "o_cT": o_cT, "o_h": o_h, "o_up": o_up, "o_y": o_y, "o_y2": o_y2})

        @block.vector
        def _(dve):
            v = nc.vector
            v.memset(QT[64:ROW_MASK, :, 0:HALF], 0.0).then_inc(s["const_v"], 1)

            def zeros(b, stage, used):
                if stage == 1:
                    v.memset(QT[64:ROW_MASK, :, HALF:T], 0.0).then_inc(s["const_v"], 1)
                    v.memset(vx[:, :, :], 0.0).then_inc(s["const_v"], 1)
                    dve.wait_ge(s["const_v"], after(3))
                    v.memset(vx[:, :, D:2 * D], 1.0).then_inc(s["const_v"], 1)

            def first_loaded(b, _, used):
                dve.wait_ge(s["first_loaded"], after(16 * len(FIRST_LOADS)))

            def ready(b, _, used):
                dve.wait_ge(s["const_v"], after(NCV))
                dve.wait_ge(s["const_p"], after(8))
                dve.wait_ge(s["w_loaded"], after(16 * len(REST_LOADS)))

            def layer_stats(n, src, st, m_v, st_sem, mv_sem, rs_sem):
                for i in range(HT):
                    v.bn_stats(st[:, i, :], src(i)).then_inc(s[st_sem], 1)
                dve.wait_ge(s[rs_sem], after(n))
                dve.wait_ge(s[st_sem], after(HT * (n + 1)))
                dve.sem_inc(s["passed"], 1)
                for i in range(HT):
                    v.bn_aggr(m_v[:, i, :], st[:, i, :]).then_inc(s[mv_sem], 1)

            def a_stat(b, c, used):
                u = 2 * b + c
                dve.wait_ge(s[f"x_loaded{c}"], after(16 * (b + 1)))
                layer_stats(u, lambda i: xt[:, c, i, :], stat, mv[:, c, :, :], "a_stat", "a_mv", "a_rstd")

            def a_q(w, dst, done):
                def item(b, c, used):
                    u = 2 * b + c
                    dve.wait_ge(s["q_sum"], after(u))
                    dve.wait_ge(s["x_written"], after(used + 1))
                    v.scalar_tensor_tensor(out=dst[:, :], in0=psX[:, :], scalar=bq[:, w:w + 1],
                                           in1=ropq[:, w, HALF * c:HALF * (c + 1)], op0=ALU.add, op1=ALU.mult
                                           ).then_inc(s["x_read"], 1)
                    dve.wait_ge(s["x_read"], after(used + 1))
                    dve.sem_inc(s[done], 1)
                return item

            def a_kv(b, c, used):
                kv = psX[:, 0:3 * D * HT].rearrange("p (i w d) -> p w i d", w=3, d=D)
                u = 2 * b + c
                n = 7 * u
                i0 = HT * c

                def bias(w):
                    return bkv[:, w, :].unsqueeze(1).to_broadcast([P, HT, D])

                dve.wait_ge(s["x_written"], after(used + 1))
                v.tensor_tensor(ka[:, :, :], kv[:, 0], bias(0), ALU.add).then_inc(s["k_steps"], 1)
                v.tensor_tensor(kb[:, :, :], kv[:, 1], bias(1), ALU.add).then_inc(s["k_steps"], 1)
                dve.wait_ge(s["vx_done"], after(2 * b))
                v.tensor_tensor(vn[:, i0:i0 + HT, :], kv[:, 2], bias(2), ALU.add).then_inc(s["vn_done"], 1)
                dve.wait_ge(s["vn_done"], after(u + 1))
                dve.sem_inc(s["x_read"], 1)
                dve.wait_ge(s["k_steps"], after(n + 2))
                v.tensor_tensor(ka[:, :, :], ka[:, :, :], ropk[:, 0, i0:i0 + HT, :], ALU.mult).then_inc(s["k_steps"], 1)
                v.tensor_tensor(kb[:, :, :], kb[:, :, :], ropk[:, 1, i0:i0 + HT, :], ALU.mult).then_inc(s["k_steps"], 1)
                dve.wait_ge(s["k_steps"], after(n + 4))
                v.tensor_tensor(kr[:, :, :], ka[:, :, :], kb[:, :, :], ALU.add).then_inc(s["k_steps"], 1)

                def part(k):
                    return kp[:, :, :, k, :]

                def thrice(t):
                    return t[:, :, :].unsqueeze(2).to_broadcast([P, HT, PARTS, D])

                dve.wait_ge(s["k_steps"], after(n + 5))
                v.tensor_copy(part(0), thrice(kr)).then_inc(s["kp_done"], 1)
                dve.wait_ge(s["kp_done"], after(3 * u + 1))
                v.tensor_tensor(ka[:, :, :], kr[:, :, :], kp[:, :, 0, 0, :], ALU.subtract).then_inc(s["k_steps"], 1)
                dve.wait_ge(s["k_steps"], after(n + 6))
                v.tensor_copy(part(1), thrice(ka)).then_inc(s["kp_done"], 1)
                dve.wait_ge(s["kp_done"], after(3 * u + 2))
                v.tensor_tensor(part(2), thrice(ka), part(1), ALU.subtract).then_inc(s["kp_done"], 1)
                dve.sem_inc(s["k_steps"], 1)

            def keys(b, c, used):
                dve.wait_ge(s["pv_done"], after(NSTEP * (b - 1) + (NSTEP if c else LAST_OF_HALF + 1)))
                dve.wait_ge(s["vn_done"], after(2 * b + c + 1))
                i = slice(HT * c, HT * (c + 1))
                v.tensor_copy(vx[:, i, 0:D], vn[:, i, :]).then_inc(s["vx_done"], 1)
                dve.wait_ge(s["KN_done"], after(2 * b + c + 1))
                t = slice(HALF * c, HALF * (c + 1))
                for w in range(NV):
                    v.tensor_copy(KT[0:ROW_MAX, w, t], KN[0:ROW_MAX, t]).then_inc(s["KT_done"], 1)

            def max_piece(b, n, used):
                i, heads, lo, hi = PIECES[n]
                dve.wait_ge(s["m_ps"], after(NPIECE * b + n + 1))
                cut = nmx[:, i, :] if i < BT else nmx2[:, i - BT, lo // BANK, :]
                v.tensor_reduce(cut[:, heads[0]:heads[-1] + 1],
                                psM[:, n % 2, 0:len(heads) * (hi - lo)].rearrange("p (h k) -> p h k", h=len(heads)),
                                AX.X, ALU.max, negate=True).then_inc(s["m_max"], 1)
                if n == OF_TILE[i][-1]:
                    dve.wait_ge(s["m_max"], after(NPIECE * b + n + 1))
                    if i < BT:
                        dve.sem_inc(s["m_block"], 1)
                    else:
                        v.tensor_tensor(nmx[:, i, :], nmx2[:, i - BT, 0, :], nmx2[:, i - BT, 1, :],
                                        ALU.min).then_inc(s["m_block"], 1)

            def turn_max(b, i, used):
                dve.wait_ge(s["nm_steps"], after(4 * (NT * b + i - 1)))
                dve.wait_ge(s["x_written"], after(used + 1))
                v.tensor_copy(nm[:, i % 2, :], psX[0:H, 0:P]).then_inc(s["x_read"], 1)
                dve.wait_ge(s["x_read"], after(used + 1))
                dve.sem_inc(s["nm_copied"], 1)

            def o_div(b, c, used):
                u = 2 * b + c
                dve.wait_ge(s["inv_written"], after(16 * u))
                dve.wait_ge(s["den_read"], after(16 * (u + 1)))
                v.reciprocal(di[:, :], dn[:, :]).then_inc(s["den_inv"], 1)

            def o_aT(b, c, used):
                u = 2 * b + c
                dve.wait_ge(s["num_read"], after(16 * (u + 1)))
                dve.wait_ge(s["inv_read"], after(16 * (u + 1)))
                v.tensor_tensor(aT[:, :], oT[:, c, :], dT[:, :], ALU.mult).then_inc(s["aT_done"], 1)

            def o_proj(b, c, used):
                dve.wait_ge(s[f"stored{c}"], after(16 * b))
                dve.wait_ge(s["x_written"], after(used + 1))
                v.tensor_tensor(y[:, c, :, :], psX[:, :].rearrange("p (i n) -> p i n", n=C),
                                bo[:, :].unsqueeze(1).to_broadcast([P, HT, C]), ALU.add).then_inc(s["x_read"], 1)
                dve.wait_ge(s["x_read"], after(used + 1))

            def o_st2(b, c, used):
                u = 2 * b + c
                layer_stats(3 * u, lambda i: y[:, c, i, :], ostat, omv, "o_stat", "o_mv", "o_rstd")

            def o_st3(b, c, used):
                u = 2 * b + c
                dve.wait_ge(s["x1_done"], after(u + 1))
                layer_stats(3 * u + 1, lambda i: x1[:, c, i, :], ostat, omv, "o_stat", "o_mv", "o_rstd")

            def o_rt(b, c, used):
                u = 2 * b + c
                dve.wait_ge(s["x_written"], after(used + 1))
                v.tensor_copy(lg[:, :, :], psX[:, 0:G * HT].rearrange("p (i e) -> p i e", e=G)).then_inc(s["x_read"], 1)
                dve.wait_ge(s["x_read"], after(used + 1))
                v.tensor_reduce(red[:, :, 0], lg[:, :, 0:E], AX.X, ALU.max).then_inc(s["rt_steps"], 1)
                dve.wait_ge(s["rt_steps"], after(17 * u + 1))
                v.tensor_tensor(ls[:, :, :], lg[:, :, 0:E], red[:, :, :].to_broadcast([P, HT, E]),
                                ALU.subtract).then_inc(s["ls_done"], 1)

            def o_top(b, c, used):
                u = 2 * b + c
                step = [1]

                def then(ins):
                    ins.then_inc(s["rt_steps"], 1)
                    step[0] += 1
                    dve.wait_ge(s["rt_steps"], after(17 * u + step[0]))

                def wide(t):
                    return t[:, :, :].to_broadcast([P, HT, E])

                dve.wait_ge(s["ex_done"], after(2 * u + 2))
                then(v.tensor_reduce(red[:, :, 0], ex[:, :, :], AX.X, ALU.add))
                then(v.reciprocal(red[:, :, :], red[:, :, :]))
                then(v.tensor_tensor(pr[:, :, :], ex[:, :, :], wide(red), ALU.mult))
                then(v.tensor_reduce(red[:, :, 0], pr[:, :, :], AX.X, ALU.max))
                then(v.tensor_tensor(eq[:, :, :], pr[:, :, :], wide(red), ALU.is_equal))
                then(v.tensor_tensor(cand[:, :, :], eq[:, :, :], rank[:, :, :], ALU.mult))
                then(v.tensor_reduce(red[:, :, 0], cand[:, :, :], AX.X, ALU.max))
                then(v.tensor_tensor(oh1[:, :, :], cand[:, :, :], wide(red), ALU.is_equal))
                then(v.scalar_tensor_tensor(out=p2[:, :, :], in0=oh1[:, :, :], scalar=-2.0, in1=pr[:, :, :],
                                            op0=ALU.mult, op1=ALU.add))
                then(v.tensor_reduce(red[:, :, 0], p2[:, :, :], AX.X, ALU.max))
                then(v.tensor_tensor(eq[:, :, :], p2[:, :, :], wide(red), ALU.is_equal))
                then(v.tensor_tensor(cand[:, :, :], eq[:, :, :], rank[:, :, :], ALU.mult))
                then(v.tensor_reduce(red[:, :, 0], cand[:, :, :], AX.X, ALU.max))
                then(v.tensor_tensor(oh2[:, :, :], cand[:, :, :], wide(red), ALU.is_equal))
                then(v.tensor_tensor(oh1[:, :, :], oh1[:, :, :], oh2[:, :, :], ALU.add))
                then(v.tensor_scalar(eg[:, :], eg[:, :], 1.0, 2.0, ALU.add, ALU.mult))
                assert step[0] == 17
                v.reciprocal(cmb[:, E, :], eg[:, :]).then_inc(s["cmb_done"], 1)
                v.scalar_tensor_tensor(out=cmb[:, 0:E, :].rearrange("p e i -> p i e"), in0=pr[:, :, :], scalar=0.5,
                                       in1=oh1[:, :, :], op0=ALU.mult, op1=ALU.mult).then_inc(s["cmb_done"], 1)

            def gated(u, e, dst):
                dve.wait_ge(s["hs_done"], after(G * u + e - SLOTS + 1))
                dve.wait_ge(s["th_done"], after(G * u + e + 1))
                v.scalar_tensor_tensor(out=dst, in0=th[:, e % SLOTS, :], scalar=1.0, in1=hidden_bank(u, e)[0],
                                       op0=ALU.add, op1=ALU.mult).then_inc(s["h_read"], 1)
                dve.wait_ge(s["h_read"], after((G + 1) * u + e + 1))
                dve.sem_inc(s["sg_done"], 1)

            def o_g(b, ce, used):
                c, e = ce
                u = 2 * b + c
                if e < E:
                    gated(u, e, hg[:, e % SLOTS, :])
                    dve.sem_inc(s["hg_done"], 1)
                else:
                    gated(u, e, shd[:, :])

            def o_up(b, c, used):
                u = 2 * b + c
                dve.wait_ge(s["h_written"], after((G + 1) * (u + 1)))
                v.tensor_tensor(hg[:, E % SLOTS, :], shd[:, :], hidden_bank(u, G)[0], ALU.mult).then_inc(s["h_read"], 1)
                dve.wait_ge(s["h_read"], after((G + 1) * (u + 1)))
                dve.sem_inc(s["hg_done"], 1)

            def o_w(b, ce, used):
                c, e = ce
                k = G * (2 * b + c) + e
                if is_last(2 * b + c):
                    dve.wait_ge(s["ye_ps"], after(k - SLOTS + 1))
                    dve.wait_ge(s["cb_done"], after(k + 1))
                    dve.wait_ge(s["hg_done"], after(k + 1))
                    v.tensor_tensor(hs[:, e % SLOTS, :], hg[:, e % SLOTS, :], cb[:, e % SLOTS, :],
                                    ALU.mult).then_inc(s["hs_done"], 1)

            def o_st4(b, c, used):
                u = 2 * b + c
                dve.wait_ge(s["ye_ps"], after(G * (u + 1)))
                layer_stats(3 * u + 2, lambda i: psY[:, P * i:P * (i + 1)], ostat, omv, "o_stat", "o_mv", "o_rstd")

            follow(dve, {"zeros": zeros, "first_loaded": first_loaded, "ready": ready,
                         "a_stat": a_stat, "a_q_out": a_q(0, qa, "qa_done"), "a_qs_out": a_q(1, qb, "qb_done"),
                         "a_kv_out": a_kv, "keys": keys, "M": max_piece, "T_out": turn_max, "o_div": o_div, "o_aT": o_aT,
                         "o_proj_out": o_proj, "o_st2": o_st2, "o_st3": o_st3, "o_rt_out": o_rt,
                         "o_top": o_top, "o_g": o_g, "o_gu": o_up, "o_w": o_w, "o_st4": o_st4})


def rope_tables():
    pos = np.arange(T, dtype=np.float32)
    freqs = (np.float32(1.0) / np.float32(10000.0) ** (np.arange(0, D, 2, dtype=np.float32) / np.float32(D))).astype(np.float32)
    ang = (pos[:, None] * freqs[None, :]).astype(np.float32)
    sin, cos = np.sin(ang), np.cos(ang)
    c = np.concatenate([cos, -cos], 1)
    n = np.concatenate([sin, sin], 1)
    q = np.stack([np.tile(c.T, (H, 1)), np.tile(n.T, (H, 1))], 1)
    k = np.stack([c.reshape(NT, P, D).transpose(1, 0, 2), n.reshape(NT, P, D).transpose(1, 0, 2)], 1)
    return np.ascontiguousarray(q, np.float32), np.ascontiguousarray(k, np.float32)


def kernel(L0_attn_x, L0_attn_Wq, L0_attn_bq, L0_attn_Wk, L0_attn_bk, L0_attn_Wv, L0_attn_bv, L0_attn_Wo, L0_attn_bo,
           L0_ffn_router_w, L0_ffn_w1, L0_ffn_w2, L0_ffn_shared_gate_up, L0_ffn_shared_down, L0_ffn_shared_gate_w):
    import concourse.bacc as bacc
    from concourse.bass_utils import run_bass_kernel_spmd

    def swap(w):
        w = np.asarray(w)
        return w.reshape(*w.shape[:-1], -1, 2, D // 2)[..., ::-1, :].reshape(w.shape)

    rope_q, rope_k = rope_tables()
    bkv = np.concatenate([np.asarray(L0_attn_bk), swap(L0_attn_bk), np.asarray(L0_attn_bv)]).reshape(1, 3, D)
    arrays = {
        "x": L0_attn_x,
        "w_in": np.concatenate([L0_attn_Wq, swap(L0_attn_Wq), L0_attn_Wk, swap(L0_attn_Wk), L0_attn_Wv], 1),
        "w_out": L0_attn_Wo,
        "b_q": np.stack([np.asarray(L0_attn_bq), swap(L0_attn_bq)], 1),
        "b_kv": np.broadcast_to(bkv, (P, 3, D)),
        "b_o": np.broadcast_to(np.asarray(L0_attn_bo)[None], (P, C)),
        "rope_q": rope_q,
        "rope_k": rope_k,
        "w_router": np.concatenate([L0_ffn_router_w, L0_ffn_shared_gate_w], 1),
        "w_up": L0_ffn_w1,
        "w_down": L0_ffn_w2,
        "w_gu": L0_ffn_shared_gate_up,
        "w_sd": L0_ffn_shared_down,
    }
    arrays = {n: np.ascontiguousarray(a) for n, a in arrays.items()}
    nc = bacc.Bacc("TRN2", target_bir_lowering=False, num_devices=1)
    args = [nc.dram_tensor(n, a.shape, F32, kind="ExternalInput").ap() for n, a in arrays.items()]
    out = nc.dram_tensor("out", (B, T, C), F32, kind="ExternalOutput").ap()
    build(nc, *args, out)
    r = run_bass_kernel_spmd(nc, [arrays], core_ids=[0])
    return r.results[0]["out"]
```
